# Optimizing a Trainium2 kernel written in Bass

```python
import numpy as np
import jax
import jax.numpy as jnp

def _softmax(x, axis=-1):
    return jax.nn.softmax(x, axis=axis)

def _gelu(x):
    return jax.nn.gelu(x, approximate=True)

def _silu(x):
    return jax.nn.silu(x)

def _sigmoid(x):
    return jax.nn.sigmoid(x)

def _layernorm(x, axis=-1, eps=1e-05):
    m = jnp.mean(x, axis=axis, keepdims=True)
    v = jnp.var(x, axis=axis, keepdims=True)
    return (x - m) / jnp.sqrt(v + eps)

def _scatter_add(tgt, idx, src, axis=0):
    return tgt.at[idx].add(src)

def _segment_sum(src, seg, n):
    return jax.ops.segment_sum(src, seg, n)
kernel_name = 'mk_prb_d1_jaxref_r2_887869'

def setup_inputs(seed: int=0):
    np.random.seed(seed)
    _w = jnp.asarray

    def _L0_attn_setup():
        import jax, jax.numpy as jnp
        import numpy as np
        HIDDEN = 1024
        NUM_HEADS = 16
        HEAD_DIM = HIDDEN // NUM_HEADS
        key = jax.random.key(seed)
        ks = jax.random.split(key, 5)
        B, S, H = (2, 1024, HIDDEN)
        qkv_bound = float(np.sqrt(6.0 / (H + 3 * H)))
        out_bound = float(np.sqrt(6.0 / (H + H)))
        return {'x': jax.random.normal(ks[0], (B, S, H), dtype=jnp.float32), 'W_qkv': jax.random.uniform(ks[1], (3 * H, H), minval=-qkv_bound, maxval=qkv_bound, dtype=jnp.float32), 'b_qkv': jnp.zeros((3 * H,), dtype=jnp.float32), 'W_out': jax.random.uniform(ks[2], (H, H), minval=-out_bound, maxval=out_bound, dtype=jnp.float32), 'b_out': jnp.zeros((H,), dtype=jnp.float32)}
    _L0_attn_in = _L0_attn_setup()

    def _L0_ffn_setup():
        import jax, jax.numpy as jnp
        import numpy as np
        FP8 = jnp.float8_e4m3fn
        key = jax.random.key(seed)
        k1, k2 = jax.random.split(key)
        input1 = jax.random.normal(k1, (2, 2048, 1024), dtype=jnp.float32)
        input2 = jax.random.normal(k2, (1024, 1024), dtype=jnp.float32)
        scale = jnp.array(0.5, dtype=jnp.float32)
        scale1 = jnp.array(0.5, dtype=jnp.float32)
        return {'input1': input1, 'input2': input2, 'scale': scale, 'scale1': scale1}
    _L0_ffn_in = _L0_ffn_setup()
    _d = {'L0_attn_x': _L0_attn_in['x'], 'L0_attn_W_qkv': _L0_attn_in['W_qkv'], 'L0_attn_b_qkv': _L0_attn_in['b_qkv'], 'L0_attn_W_out': _L0_attn_in['W_out'], 'L0_attn_b_out': _L0_attn_in['b_out'], 'L0_ffn_input2': _L0_ffn_in['input2'], 'L0_ffn_scale': _L0_ffn_in['scale'], 'L0_ffn_scale1': _L0_ffn_in['scale1']}
    _x0 = _d['L0_attn_x']
    _d['L0_attn_x'] = jax.random.normal(jax.random.fold_in(jax.random.key(seed), 1), (4, 1024, 1024), dtype=_x0.dtype)
    del _x0
    return _d

def reference(L0_attn_x, L0_attn_W_qkv, L0_attn_b_qkv, L0_attn_W_out, L0_attn_b_out, L0_ffn_input2, L0_ffn_scale, L0_ffn_scale1):

    def _L0_attn_ref(x, W_qkv, b_qkv, W_out, b_out):
        import jax, jax.numpy as jnp
        import numpy as np
        HIDDEN = 1024
        NUM_HEADS = 16
        HEAD_DIM = HIDDEN // NUM_HEADS
        B, S, H = x.shape
        qkv = x @ W_qkv.T + b_qkv
        q, k, v = jnp.split(qkv, 3, axis=-1)

        def to_heads(t):
            return t.reshape(B, S, NUM_HEADS, HEAD_DIM).transpose(0, 2, 1, 3)
        q, k, v = (to_heads(q), to_heads(k), to_heads(v))
        scale = HEAD_DIM ** (-0.5)
        scores = jnp.einsum('bnqd,bnkd->bnqk', q, k) * scale
        causal = jnp.triu(jnp.ones((S, S), dtype=bool), k=1)
        scores = jnp.where(causal, -jnp.inf, scores)
        attn = jax.nn.softmax(scores, axis=-1)
        out = jnp.einsum('bnqk,bnkd->bnqd', attn, v)
        out = out.transpose(0, 2, 1, 3).reshape(B, S, H)
        return out @ W_out.T + b_out

    def _L0_ffn_ref(input1, input2, scale, scale1):
        import jax, jax.numpy as jnp
        import numpy as np
        FP8 = jnp.float8_e4m3fn
        q1 = (input1 * scale).astype(FP8)
        q2 = (input2 * scale1).astype(FP8)
        d1 = q1.astype(jnp.float32) * (1.0 / scale)
        d2 = q2.astype(jnp.float32) * (1.0 / scale1)
        return jnp.einsum('bmk,kn->bmn', d1, d2)
    x = L0_attn_x
    xn = _layernorm(x, axis=-1)
    x = x + _L0_attn_ref(xn, L0_attn_W_qkv, L0_attn_b_qkv, L0_attn_W_out, L0_attn_b_out) + _L0_ffn_ref(xn, L0_ffn_input2, L0_ffn_scale, L0_ffn_scale1)
    return x

_drawn_inputs = setup_inputs


def setup_inputs(seed=0):
    import zlib

    import numpy as np

    out = dict(_drawn_inputs(seed))
    spreads = {'L0_attn_b_qkv': (0.0, 0.8), 'L0_attn_b_out': (0.0, 2.0)}
    factors = {'L0_attn_W_qkv': 8.0, 'L0_attn_W_out': 8.0}
    for name, (base, spread) in spreads.items():
        noise = np.random.default_rng([zlib.crc32(name.encode()), seed]).standard_normal(out[name].shape)
        drawn = base * np.exp(spread * noise) if base else spread * noise
        out[name] = jnp.asarray(drawn.astype(out[name].dtype))
    for name, factor in factors.items():
        out[name] = (out[name] * factor).astype(out[name].dtype)
    return out
```

```python
import concourse.bass as bass
from concourse import mybir
from contextlib import ExitStack

B, S, H = 4, 1024, 1024
HEADS, D = 16, 64
PAIRS = HEADS // 2
T = 128
NT = S // T
CH = 512
VW = 2 * D + 2

ST_UNITS = [
    [(0, 0, 512)],
    [(1, 128, 384), (3, 384, 128)],
    [(2, 256, 256), (6, 768, 256)],
    [(0, 512, 512)], [(1, 512, 512)], [(2, 512, 512)], [(3, 512, 512)],
    [(4, 512, 512)],
    [(5, 640, 384), (7, 896, 128)],
]
MAX_UNITS = [
    [(0, 0, 128), (2, 0, 384)],
    [(1, 0, 256), (5, 512, 256)],
    [(3, 0, 512)],
    [(4, 0, 512)],
    [(4, 512, 128), (6, 512, 384)],
    [(5, 0, 512)],
    [(6, 0, 512)],
    [(7, 0, 512)],
    [(7, 512, 512)],
]
NU = len(ST_UNITS)
SEGS = 4


def block_at(kb, qt):
    for u, parts in enumerate(ST_UNITS):
        off = 0
        for k, q0, w in parts:
            if k == kb and q0 <= qt * T < q0 + w:
                return u, off + qt * T - q0
            off += w
    raise ValueError((kb, qt))


def pair_steps(with_next, first_pair=False):
    proj = [("proj", n, s) for n in range(4) for s in range(SEGS)] if with_next else []
    maxi = []
    if with_next:
        for h in range(2):
            maxi += [("max", h, u) for u in range(NU)] + [("mt", h, 0)]
    out = [("st", 0, 0), ("st", 0, 1)]
    att = [("st", 0, 2), ("st", 0, 3), ("st", 0, 4), ("pv", 0, 0), ("st", 0, 5), ("pv", 0, 1)]
    att += [("st", 0, 6), ("st", 0, 7), ("st", 0, 8), ("st", 1, 0), ("st", 1, 1), ("pv", 0, 2), ("pv", 0, 3)]
    att += [("st", 1, 2), ("st", 1, 3), ("st", 1, 4), ("pv", 1, 0), ("st", 1, 5), ("pv", 1, 1)]
    att += [("st", 1, 6), ("st", 1, 7), ("st", 1, 8)]
    tail = [("pv", 1, 2), ("pv", 1, 3)]
    while att or proj:
        if proj:
            out.append(proj.pop(0))
        if att:
            out.append(att.pop(0))
    k = 0
    for m in maxi:
        out.append(m)
        k += 1
        if tail and k in (2, 4, 6, 8):
            out.append(tail.pop(0))
    return out + tail + [("ot", 0, 0), ("ot", 1, 0), ("ot", 2, 0)]


OT_TILES = [(0, 3), (3, 3), (6, 2)]

W_PRO = 1 + 2 * 32
U_X, U_F, U_V = 3 * NT, 2 * NT, 2 * NT
U_NEXT = 4 + 2 * (NU + 1)
U_PAIR = U_NEXT + 3
AT_F = U_X
AT_V = AT_F + U_F
AT_P0 = AT_V + U_V
AT_PAIRS = AT_P0 + U_NEXT
AT_OUT = AT_PAIRS + (PAIRS - 1) * U_PAIR + 3
W_BATCH = AT_OUT + 2 * NT
assert U_PAIR % 3 == 0 and W_BATCH % 3 == 0

SHIFT = 32768.0
NEG = -1.0e30


def block_kernel(nc, x, w_qkv, b_qkv, w_out, b_out, w2, scale, scale1, out):
    fp32, f16, bf16 = mybir.dt.float32, mybir.dt.float16, mybir.dt.bfloat16
    u32 = mybir.dt.uint32
    ALU = mybir.AluOpType
    ACT = mybir.ActivationFunctionType
    AX = mybir.AxisListType

    wqk_d = nc.dram_tensor("wqk_split", (PAIRS, T, 4 * NT * T), f16, kind="Internal").ap()
    wv_d = nc.dram_tensor("wv_split", (NT, T, 2 * NT * T), f16, kind="Internal").ap()
    w2_d = nc.dram_tensor("w2_quantised", (NT, T, H), bf16, kind="Internal").ap()
    y_d = nc.dram_tensor("ffn_part", (B * NT, T, H), fp32, kind="Internal").ap()
    x_t = x.rearrange("b (t p) h -> (b t) p h", p=T)
    out_t = out.rearrange("b (t p) h -> (b t) p h", p=T)

    ctx = ExitStack()
    with ctx:
        def sem(name):
            return ctx.enter_context(nc.semaphore(name))

        def small(name, shape, dt):
            return ctx.enter_context(nc.sbuf_tensor(name, shape, dt))

        xs_r = small("xs_region", [T, 8192], fp32)
        v_r = small("v_region", [T, NT * HEADS * VW // 2], fp32)
        w_r = small("wqk_region", [T, 4096], fp32)
        s_r = small("stack_region", [T, 8192], fp32)
        p_r = small("p_region", [T, NU * CH], fp32)
        o_r = small("ot_region", [T, 8192], fp32)
        wo_r = small("wo_region", [T, 8192], fp32)
        ost = small("o_rows", [T, NT, T], fp32)
        stage = small("qk_stage", [T, 2, 2, CH], f16)
        m_hl = small("max_rows", [NT, 2, 2, T], f16)
        ident = small("ident", [T, T], fp32)
        identb = small("identb", [T, T], bf16)
        maskb = small("mask_future", [T, T], bf16)
        pv_lo = small("pv_lo", [T, 2, 2, D], fp32)
        pv_num = small("pv_num", [T, 2, 2, D], fp32)
        pv_rec = small("pv_rec", [T, 2, 2, 1], fp32)
        m_part = small("max_parts", [T, 2, NT, 2], fp32)
        m_neg = small("max_negated", [T, 2, NT], fp32)
        bias = small("biases", [T, 3, NT], fp32)
        sc = small("scalars", [T, 72], fp32)

        xs = xs_r[:, :].bitcast(f16).rearrange("p (l k t) -> p l k t", l=2, k=NT)
        V = v_r[:, :].bitcast(f16).rearrange("p (t h w) -> p t h w", t=NT, h=HEADS)
        wqk = w_r[:, :].bitcast(f16).rearrange("p (s q l k f) -> p s q l k f", s=2, q=2, l=2, k=NT)
        w2q = w_r[:, :].bitcast(bf16).rearrange("p (k n) -> p k n", k=NT)
        P = p_r[:, :].bitcast(f16).rearrange("p (u l q) -> p u l q", u=NU, l=2)
        xq = p_r[:, 0:4096].bitcast(bf16).rearrange("p (k t) -> p k t", k=NT)
        OT = o_r[:, :].bitcast(f16).rearrange("p (l g t) -> p l g t", l=2, g=PAIRS)
        WV = o_r[:, :].bitcast(f16).rearrange("p (g l k f) -> p g l k f", g=NT, l=2, k=NT)
        WO = wo_r[:, :].bitcast(f16).rearrange("p (l k n) -> p l k n", l=2, k=NT)

        stk = s_r[:, :].bitcast(f16).rearrange("p (r w t) -> p r w t", r=2, w=8)
        QA = [[stk[:, r, 2 * h, :] for h in range(2)] for r in range(2)]
        QB = [[stk[:, r, 2 * h + 1, :] for h in range(2)] for r in range(2)]
        KA = [[stk[:, r, 4 + h, :] for h in range(2)] for r in range(2)]
        KB = [[stk[:, r, 6 + h, :] for h in range(2)] for r in range(2)]

        xt = [s_r[:, 1024 * i:1024 * i + 1024] for i in range(2)]
        xqt = s_r[:, 2048:2560].bitcast(bf16)
        qy, qm, qq = (s_r[:, 4096 + 1024 * i:5120 + 1024 * i] for i in range(3))
        bout = s_r[:, 4096:5120]
        yst = [s_r[:, 5120 + 512 * i:5632 + 512 * i] for i in range(2)]

        raw = ([xs_r[:, 1024 * i:1024 * i + 1024] for i in range(8)]
               + [v_r[:, 1024 * i:1024 * i + 1024] for i in range(8)]
               + [s_r[:, 1024 * i:1024 * i + 1024] for i in range(8)]
               + [o_r[:, 1024 * i:1024 * i + 1024] for i in range(8)])
        w2t = [wo_r[:, 1024 * i:1024 * i + 1024] for i in range(2)]
        w2y, w2m, w2q32 = (wo_r[:, 2048 + 1024 * i:3072 + 1024 * i] for i in range(3))
        w2b = [wo_r[:, 5120 + 512 * i:5632 + 512 * i].bitcast(bf16) for i in range(2)]
        wv_stage = p_r[:, 0:4096].bitcast(f16).rearrange("p (s l k f) -> p s l k f", s=4, l=2, k=NT)

        col = {}

        def s_(name, n=1):
            if name not in col:
                col[name] = (sum(w for _, w in col.values()), n)
            a, w = col[name]
            return sc[:, a:a + w]

        WK = [ctx.enter_context(nc.psum_tensor(f"work{i}", [T, CH], fp32)) for i in range(3)]
        ST = [ctx.enter_context(nc.psum_tensor(f"scores{i}", [T, CH], fp32)) for i in range(3)]
        PV = [ctx.enter_context(nc.psum_tensor(f"pv{i}", [T, CH], fp32)) for i in range(2)]

        work_full = sem("work_full")
        work_hi = sem("work_hi")
        work_free = sem("work_free")
        st_full = sem("st_full")
        st_exp = sem("st_exp")
        st_free = sem("st_free")
        pv_full = sem("pv_full")
        pv_half = sem("pv_half")
        pv_free = sem("pv_free")
        o_done = sem("o_done")
        m_ready = sem("m_ready")
        stage_dma = [sem(f"stage_dma{i}") for i in range(2)]
        m_dma = [sem(f"m_dma{i}") for i in range(2)]
        w_dma = [sem(f"w_dma{i}") for i in range(2)]
        x_dma = [sem(f"x_dma{i}") for i in range(2)]
        xf_dma = [sem(f"xf_dma{i}") for i in range(2)]
        y_dma = [sem(f"y_dma{i}") for i in range(2)]
        y_st = [sem(f"y_st{i}") for i in range(2)]
        out_st = [sem(f"out_st{i}") for i in range(2)]
        wv_dma, w2q_dma, bout_dma = sem("wv_dma"), sem("w2q_dma"), sem("bout_dma")
        raw_dma = [sem(f"raw_dma{i}") for i in range(4)]
        misc_dma = sem("misc_dma")
        w2_dma = sem("w2_dma")
        w2_st = sem("w2_st")
        wqk_st = [sem(f"wqk_st{i}") for i in range(2)]
        wv_st = [sem(f"wv_st{i}") for i in range(4)]
        consts = sem("consts")
        gmax = sem("gmax")
        mx_ready = sem("mx_ready")
        sc_ready = sem("sc_ready")
        held = sem("held")
        dve = sem("dve")
        pool = sem("pool")
        var_ready, rstd_ready = sem("var_ready"), sem("rstd_ready")
        xn_ready = sem("xn_ready")
        q_m, q_q, q_z, q_done = sem("q_m"), sem("q_q"), sem("q_z"), sem("q_done")
        xb_ready = sem("xb_ready")

        class Chain:

            def __init__(self, eng, s):
                self.eng, self.s, self.base, self.n = eng, s, 0, 0

            def step(self, ins):
                ins.then_inc(self.s, 1)
                self.n += 1
                self.eng.wait_ge(self.s, self.base + self.n)

        def until(eng, s, value):
            eng.wait_ge(s, value)
            eng.sem_inc(held, 1)

        block = ctx.enter_context(nc.Block())

        @block.sync
        def _(sp):
            sp.dma_start(ost[0:24, 0, :], b_qkv.rearrange("(a p) -> a p", p=T)).then_inc(misc_dma, 16)
            sp.dma_start(s_("scale"), scale.to_broadcast((T, 1))).then_inc(misc_dma, 16)
            sp.dma_start(s_("scale1"), scale1.to_broadcast((T, 1))).then_inc(misc_dma, 16)
            for g in range(4):
                src = w_qkv[g * 1024:(g + 1) * 1024, :] if g < 3 else w_out
                for i in range(NT):
                    sp.dma_start(raw[8 * g + i], src[i * T:(i + 1) * T, :]).then_inc(raw_dma[g], 16)
            with sp.Fori(0, NT) as t:
                until(sp, w2_st, 16 + t * 16)
                sp.dma_start(w2t[0], w2.rearrange("(k p) n -> k p n", p=T)[t, :, :]).then_inc(w2_dma, 16)
                until(sp, q_done, t + 1)
                sp.dma_start(w2_d[t, :, :], w2b[0]).then_inc(w2_st, 16)
            for p in range(PAIRS):
                sp.wait_ge(work_free, 3 + 17 + 6 * p + 4)
                sp.dma_start(wqk_d[p, :, :], w_r[:, 2048 * (p % 2):2048 * (p % 2) + 2048].bitcast(f16))\
                  .then_inc(wqk_st[p % 2], 16)
                sp.wait_ge(work_free, 3 + 17 + 6 * p + 6)
                sp.dma_start(wv_d[p, :, :], p_r[:, 1024 * (p % 4):1024 * (p % 4) + 1024].bitcast(f16))\
                  .then_inc(wv_st[p % 4], 16)
            sp.wait_ge(w2_st, 16 + 16 * NT)
            for q in wqk_st:
                sp.wait_ge(q, 16 * PAIRS // 2)
            for q in wv_st:
                sp.wait_ge(q, 16 * PAIRS // 4)

            def stacks(n, r, k):
                s, c = n % 2, slice((n % 2) * CH, (n % 2) * CH + CH)
                until(sp, work_free, k)
                for h in range(2):
                    hi, lo = stage[D * h:D * h + D, s, 0, :], stage[D * h:D * h + D, s, 1, :]
                    if n < 2:
                        todo = [(QA[r][h][0:D, c], hi), (QA[r][h][D:T, c], hi), (QB[r][h][0:D, c], lo)]
                    else:
                        todo = [(KA[r][h][0:D, c], hi), (KA[r][h][D:T, c], lo), (KB[r][h][0:D, c], hi)]
                    for dst, src in todo:
                        sp.dma_start(dst, src).then_inc(stage_dma[s], 16)

            def max_rows(h, r, k):
                until(sp, work_free, k)
                for part in range(2):
                    sp.dma_start(QB[r][h][D + part:D + part + 1, :], m_hl[:, h, part, :]).then_inc(m_dma[h], 16)

            with sp.Fori(0, B) as b:
                base = b * W_BATCH + W_PRO
                until(sp, work_full, base)
                sp.dma_start(o_r[:, :].bitcast(f16).rearrange("p (g n) -> p g n", g=NT),
                             wv_d.rearrange("g p n -> p g n")).then_inc(wv_dma, 16)
                sp.dma_start(w2q, w2_d.rearrange("k p n -> p k n")).then_inc(w2q_dma, 16)
                until(sp, out_st[0], 16 + b * 64)
                until(sp, out_st[1], 16 + b * 64)
                for t in range(NT):
                    if t >= 2:
                        until(sp, work_free, base + 3 + 3 * (t - 1))
                    sp.dma_start(xt[t % 2], x_t[b * NT + t, :, :]).then_inc(x_dma[t % 2], 16)
                until(sp, work_free, base + 3 + U_X)
                sp.dma_start(bout, b_out.rearrange("(a n) -> a n", a=1).to_broadcast((T, H)))\
                  .then_inc(bout_dma, 16)
                for t in range(NT):
                    if t >= 2:
                        until(sp, work_free, base + 3 + AT_F + 2 * (t - 1))
                    sp.dma_start(xt[t % 2], x_t[b * NT + t, :, :]).then_inc(xf_dma[t % 2], 16)
                    if t >= 1:
                        for half in range(2):
                            until(sp, work_free, base + 3 + AT_F + 2 * (t - 1) + half + 1)
                            sp.dma_start(y_d[b * NT + t - 1, :, half * CH:(half + 1) * CH], yst[half])\
                              .then_inc(y_st[half], 16)
                for half in range(2):
                    until(sp, work_free, base + 3 + AT_F + 2 * (NT - 1) + half + 1)
                    sp.dma_start(y_d[b * NT + NT - 1, :, half * CH:(half + 1) * CH], yst[half])\
                      .then_inc(y_st[half], 16)
                until(sp, work_full, base + AT_V)
                for s in range(2):
                    sp.dma_start(w_r[:, 2048 * s:2048 * s + 2048].bitcast(f16), wqk_d[s, :, :])\
                      .then_inc(w_dma[s], 16)
                for half in range(2):
                    until(sp, y_st[half], 16 + (b + 1) * NT * 16)
                for n in range(4):
                    stacks(n, 0, base + 3 + AT_P0 + n + 1)
                for h in range(2):
                    max_rows(h, 0, base + 3 + AT_P0 + 4 + (h + 1) * (NU + 1))

                def pair(p, r, with_next, load):
                    at = base + 3 + AT_PAIRS + p * U_PAIR
                    if load:
                        sp.dma_start(w_r[:, 2048 * r:2048 * r + 2048].bitcast(f16), wqk_d[p + 2, :, :])\
                          .then_inc(w_dma[r], 16)
                    if with_next:
                        until(sp, st_full, 1 + (b * PAIRS + p) * 2 * NU)
                        for n in range(4):
                            stacks(n, 1 - r, at + n + 1)
                        for h in range(2):
                            max_rows(h, 1 - r, at + 4 + (h + 1) * (NU + 1))

                with sp.Fori(0, PAIRS // 2 - 1) as j:
                    for r in range(2):
                        pair(2 * j + r, r, True, True)
                pair(PAIRS - 2, 0, True, False)
                until(sp, st_full, 1 + (b * PAIRS + PAIRS - 1) * 2 * NU)
                for t in range(NT):
                    if t >= 2:
                        until(sp, out_st[t % 2], 16 + b * 64 + 16 * (t // 2))
                    sp.dma_start(xt[t % 2], y_d[b * NT + t, :, :]).then_inc(y_dma[t % 2], 16)
                    if t >= 1:
                        until(sp, work_free, base + 3 + AT_OUT + 2 * t)
                        sp.dma_start(out_t[b * NT + t - 1, :, :], xt[(t - 1) % 2]).then_inc(out_st[(t - 1) % 2], 16)
                until(sp, work_free, base + 3 + AT_OUT + 2 * NT)
                sp.dma_start(out_t[b * NT + NT - 1, :, :], xt[1]).then_inc(out_st[1], 16)
            for s in range(2):
                until(sp, out_st[s], 16 + B * 64)

        @block.tensor
        def _(pe):
            def transposes(n, free, srcs, idt, out_of):
                pe.wait_ge(work_free, free)
                for i, s in enumerate(srcs):
                    ins = pe.transpose(out_of(i), s, idt)
                ins.then_inc(work_full, 1)

            pe.wait_ge(consts, 5)
            pe.wait_ge(misc_dma, 48)
            pe.wait_ge(work_free, 1)
            pe.transpose(WK[0][:, 0:24], ost[0:24, 0, :], ident[0:24, 0:24]).then_inc(work_full, 1)
            order = list(range(24, 32))
            for p in range(PAIRS):
                order += [p, 8 + p, 16 + p]
            for i, t in enumerate(order):
                pe.wait_ge(raw_dma[t // 8], 16 * NT)
                for g in range(2):
                    n = 1 + 2 * i + g
                    bank = WK[n % 3]
                    pe.wait_ge(work_free, n + 1)
                    for k in range(4):
                        ins = pe.transpose(bank[:, k * T:(k + 1) * T],
                                           raw[t][:, (4 * g + k) * T:(4 * g + k + 1) * T], ident[:, :])
                    ins.then_inc(work_full, 1)

            with pe.Fori(0, B) as b:
                base = b * W_BATCH + W_PRO
                for t in range(NT):
                    pe.wait_ge(xn_ready, b * NT + t + 1)
                    for g in range(2):
                        n = W_PRO + 3 * t + g
                        pe.wait_ge(work_free, base + 3 * t + g + 1)
                        for k in range(4):
                            ins = pe.transpose(WK[n % 3][:, k * T:(k + 1) * T],
                                               xt[t % 2][:, (4 * g + k) * T:(4 * g + k + 1) * T], ident[:, :])
                        ins.then_inc(work_full, 1)
                    n = W_PRO + 3 * t + 2
                    pe.wait_ge(work_free, base + 3 * t + 3)
                    pe.wait_ge(q_done, NT + b * NT + t + 1)
                    tb = WK[n % 3][:, :].bitcast(bf16)
                    for k in range(NT):
                        ins = pe.transpose(tb[:, k * T:(k + 1) * T], xqt[:, k * T:(k + 1) * T], identb[:, :])
                    ins.then_inc(work_full, 1)
                pe.wait_ge(w2q_dma, (b + 1) * 16)
                pe.wait_ge(work_free, base + 3 + U_X)
                for t in range(NT):
                    for half in range(2):
                        k0 = AT_F + 2 * t + half
                        bank = WK[(W_PRO + k0) % 3]
                        pe.wait_ge(work_free, base + k0 + 1)
                        for k in range(NT):
                            ins = pe.matmul(bank[:, :], xq[:, k, t * T:(t + 1) * T],
                                            w2q[:, k, half * CH:(half + 1) * CH],
                                            start=(k == 0), stop=(k == NT - 1))
                        ins.then_inc(work_full, 1)
                pe.wait_ge(wv_dma, (b + 1) * 16)
                for t in range(NT):
                    for half in range(2):
                        k0 = AT_V + 2 * t + half
                        bank = WK[(W_PRO + k0) % 3]
                        pe.wait_ge(work_free, base + k0 + 1)
                        for k in range(NT):
                            for i, (lx, lw) in enumerate(((0, 0), (0, 1), (1, 0))):
                                ins = pe.matmul(bank[:, :], xs[:, lx, k, t * T:(t + 1) * T],
                                                WV[:, 4 * half:4 * half + 4, lw, k, :],
                                                start=(k == 0 and i == 0), stop=(k == NT - 1 and i == 2))
                        ins.then_inc(work_full, 1)

                def proj(n, seg, s, k0, free):
                    bank = WK[(W_PRO + k0) % 3]
                    kind, c = n // 2, n % 2
                    if seg == 0:
                        pe.wait_ge(work_free, free + 1)
                    for k in range(seg * NT // SEGS, (seg + 1) * NT // SEGS):
                        for i, (lw, lx) in enumerate(((0, 0), (0, 1), (1, 0))):
                            ins = pe.matmul(bank[:, :], wqk[:, s, kind, lw, k, :],
                                            xs[:, lx, k, c * CH:(c + 1) * CH],
                                            start=(k == 0 and i == 0), stop=(k == NT - 1 and i == 2))
                    if seg == SEGS - 1:
                        ins.then_inc(work_full, 1)

                def maxima(h, u, r, k0, free):
                    bank = WK[(W_PRO + k0) % 3]
                    pe.wait_ge(work_free, free + 1)
                    off = 0
                    for qt, k, w in MAX_UNITS[u]:
                        diag = k <= qt * T < k + w
                        ins = pe.matmul(bank[:, off:off + w], QA[r][h][:, qt * T:(qt + 1) * T],
                                        KA[r][h][:, k:k + w], start=True, stop=True)
                        if diag:
                            d = off + qt * T - k
                            ins = pe.matmul(bank[:, d:d + T], identb[:, :], maskb[:, :],
                                            start=False, stop=True, skip_group_check=True)
                        off += w
                    ins.then_inc(work_full, 1)

                def max_transpose(h, k0, free, ready):
                    bank = WK[(W_PRO + k0) % 3]
                    pe.wait_ge(work_free, free + 1)
                    pe.wait_ge(m_ready, ready)
                    pe.transpose(bank[0:NT, 0:T], m_neg[:, h, :], ident[:, :]).then_inc(work_full, 1)

                at = base + AT_P0
                pe.wait_ge(w_dma[0], b * (PAIRS // 2) * 16 + 16)
                for n in range(4):
                    for seg in range(SEGS):
                        proj(n, seg, 0, AT_P0 + n, at + n)
                for s in range(2):
                    pe.wait_ge(stage_dma[s], 96 + (b * PAIRS + 1) * 192)
                for h in range(2):
                    for u in range(NU):
                        k0 = 4 + h * (NU + 1) + u
                        maxima(h, u, 0, AT_P0 + k0, at + k0)
                    k0 = 4 + h * (NU + 1) + NU
                    max_transpose(h, AT_P0 + k0, at + k0, b * HEADS + h + 1)

                def pair(p, r, with_next, turn):
                    at = base + AT_PAIRS + p * U_PAIR
                    gp = b * PAIRS + p
                    k0 = 0
                    waited = False
                    for kind, a, c in pair_steps(with_next):
                        if kind == "st":
                            if c == 0:
                                pe.wait_ge(m_dma[a], 32 + (gp + 1) * 32)
                            n = a * NU + c
                            bank = ST[n % 3]
                            pe.wait_ge(st_free, gp * 2 * NU + n + 1)
                            off = 0
                            for kb, q0, w in ST_UNITS[c]:
                                pe.matmul(bank[:, off:off + w], KA[r][a][:, kb * T:(kb + 1) * T],
                                          QA[r][a][:, q0:q0 + w], start=True, stop=False)
                                ins = pe.matmul(bank[:, off:off + w], KB[r][a][0:D + 2, kb * T:(kb + 1) * T],
                                                QB[r][a][0:D + 2, q0:q0 + w], start=False, stop=True)
                                if kb * T >= q0:
                                    ins = pe.matmul(bank[:, off:off + T], maskb[:, :], identb[:, :],
                                                    start=False, stop=True, skip_group_check=True)
                                off += w
                            ins.then_inc(st_full, 1)
                        elif kind == "pv":
                            n = a * 4 + c
                            head = 2 * p + a
                            bank = PV[n % 2]
                            pe.wait_ge(st_free, 3 + (gp * 2 + a) * NU + (3 if c < 2 else NU))
                            pe.wait_ge(pv_free, gp * 8 + n + 1)
                            for i in range(2):
                                qt = 2 * c + i
                                o = i * (2 * D + 1)
                                for kb in range(qt + 1):
                                    u, q = block_at(kb, qt)
                                    pe.matmul(bank[:, o:o + 2 * D + 1], P[:, u, 0, q:q + T],
                                              V[:, kb, head, 0:2 * D + 1], start=(kb == 0), stop=False,
                                              skip_group_check=True)
                                    ins = pe.matmul(bank[:, o:o + D + 1], P[:, u, 1, q:q + T],
                                                    V[:, kb, head, 0:D + 1], start=False, stop=(kb == qt),
                                                    skip_group_check=True)
                            ins.then_inc(pv_full, 1)
                        elif kind == "proj":
                            if a == 0 and c == 0:
                                s = 1 - r
                                pe.wait_ge(w_dma[s], (b * (PAIRS // 2) + turn + 1) * 16)
                            proj(a, c, 1 - r, AT_PAIRS + k0, at + k0)
                            k0 += c == SEGS - 1
                        elif kind == "max":
                            if not waited:
                                for s in range(2):
                                    pe.wait_ge(stage_dma[s], 96 + (gp + 2) * 192)
                                waited = True
                            maxima(a, c, 1 - r, AT_PAIRS + k0, at + k0)
                            k0 += 1
                        elif kind == "mt":
                            max_transpose(a, AT_PAIRS + k0, at + k0, (gp + 1) * 2 + a + 1)
                            k0 += 1
                        elif kind == "ot":
                            if a == 0:
                                pe.wait_ge(o_done, 2 + (gp + 1) * 8)
                            t0, m = OT_TILES[a]
                            bank = WK[(W_PRO + AT_PAIRS + k0) % 3]
                            pe.wait_ge(work_free, at + k0 + 1)
                            for i in range(m):
                                ins = pe.transpose(bank[:, i * T:(i + 1) * T], ost[:, t0 + i, :], ident[:, :])
                            ins.then_inc(work_full, 1)
                            k0 += 1

                with pe.Fori(0, PAIRS // 2 - 1) as j:
                    for r in range(2):
                        pair(2 * j + r, r, True, j + r)
                pair(PAIRS - 2, 0, True, PAIRS // 2 - 1)
                pair(PAIRS - 1, 1, False, None)

                for t in range(NT):
                    for half in range(2):
                        k0 = AT_OUT + 2 * t + half
                        bank = WK[(W_PRO + k0) % 3]
                        if t == 0 and half == 0:
                            pe.wait_ge(work_free, base + 3 + AT_OUT)
                        pe.wait_ge(work_free, base + k0 + 1)
                        for k in range(PAIRS):
                            for i, (lo, lw) in enumerate(((0, 0), (0, 1), (1, 0))):
                                ins = pe.matmul(bank[:, :], OT[:, lo, k, t * T:(t + 1) * T],
                                                WO[:, lw, k, half * CH:(half + 1) * CH],
                                                start=(k == 0 and i == 0), stop=(k == PAIRS - 1 and i == 2))
                        ins.then_inc(work_full, 1)

        @block.scalar
        def _(act):
            act.wait_ge(sc_ready, 1)
            order = [(3, i) for i in range(8)]
            for p in range(PAIRS):
                order += [(0, p), (1, p), (2, p)]
            for i, (m, p) in enumerate(order):
                for g in range(2):
                    n = 1 + 2 * i + g
                    act.wait_ge(work_full, n + 1)
                    src = WK[n % 3][:, :].rearrange("p (k f) -> p k f", k=4)
                    if m == 3:
                        if i == 0 and g == 0:
                            act.wait_ge(w2_st, 16 + 16 * NT)
                        dst = WO[:, 0, 4 * g:4 * g + 4, p * T:(p + 1) * T]
                    elif m == 2:
                        if p >= 4:
                            act.wait_ge(wv_st[p % 4], 16 * (p // 4))
                        dst = wv_stage[:, p % 4, 0, 4 * g:4 * g + 4, :]
                    else:
                        if p >= 2:
                            act.wait_ge(wqk_st[p % 2], 16 * (p // 2))
                        dst = wqk[:, p % 2, m, 0, 4 * g:4 * g + 4, :]
                    act.activation(dst, src, ACT.Copy, scale=s_("w_s", 4)[:, m:m + 1]).then_inc(work_hi, 1)

            with act.Fori(0, B) as b:
                base = b * W_BATCH + W_PRO
                for t in range(NT):
                    for g in range(2):
                        n = W_PRO + 3 * t + g
                        act.wait_ge(work_full, base + 3 * t + g + 1)
                        act.activation(xs[:, 0, 4 * g:4 * g + 4, t * T:(t + 1) * T],
                                       WK[n % 3][:, :].rearrange("p (k f) -> p k f", k=4), ACT.Copy)\
                           .then_inc(work_hi, 1)
                for t in range(NT):
                    for half in range(2):
                        k0 = AT_V + 2 * t + half
                        act.wait_ge(work_full, base + k0 + 1)
                        act.activation(V[:, t, 8 * half:8 * half + 8, 0:D],
                                       WK[(W_PRO + k0) % 3][:, :].rearrange("p (h d) -> p h d", d=D),
                                       ACT.Copy, scale=s_("c_v")).then_inc(work_hi, 1)

                def proj(n, full, k0, gp, pair_col):
                    bank, s, kind = WK[(W_PRO + k0) % 3], n % 2, n // 2
                    act.wait_ge(work_full, full)
                    until(act, stage_dma[s], 96 + gp * 192 + (n // 2) * 96)
                    c = s_("c_q") if kind == 0 else s_("c_k")
                    bs = bias[:, kind, pair_col]
                    act.activation(stage[:, s, 0, :], bank[:, :], ACT.Identity, bias=bs, scale=c)
                    act.activation(bank[:, :], bank[:, :], ACT.Identity, bias=bs, scale=c).then_inc(work_hi, 1)

                def max_rows(h, full, k0, gp):
                    act.wait_ge(work_full, full)
                    act.wait_ge(m_dma[h], 32 + gp * 32)
                    act.activation(m_hl[:, h, 0, :], WK[(W_PRO + k0) % 3][0:NT, 0:T], ACT.Copy,
                                   scale=1.0 / SHIFT).then_inc(work_hi, 1)

                at = base + AT_P0
                for n in range(4):
                    proj(n, at + n + 1, AT_P0 + n, b * PAIRS, slice(0, 1))
                for h in range(2):
                    k0 = 4 + h * (NU + 1) + NU
                    max_rows(h, at + k0 + 1, AT_P0 + k0, b * PAIRS)

                def pair(p, r, with_next):
                    at = base + AT_PAIRS + p * U_PAIR
                    gp = b * PAIRS + p
                    k0 = 0
                    for kind, a, c in pair_steps(with_next):
                        if kind == "st":
                            n = a * NU + c
                            bank = ST[n % 3]
                            act.wait_ge(st_full, 1 + gp * 2 * NU + n + 1)
                            if c == 0:
                                act.wait_ge(pv_full, 2 + (gp * 2 + a) * 4)
                            if c == 2:
                                act.wait_ge(pv_full, 4 + (gp * 2 + a) * 4)
                            act.activation(P[:, c, 0, :], bank[:, :], ACT.Exp, scale=s_("e_s"))
                            act.activation(bank[:, :], bank[:, :], ACT.Exp, scale=s_("e_s")).then_inc(st_exp, 1)
                        elif kind == "pv":
                            n = a * 4 + c
                            act.wait_ge(pv_full, 4 + gp * 8 + n + 1)
                            act.wait_ge(pv_free, gp * 8 + n + 1)
                            src = PV[n % 2][:, 0:2 * (2 * D + 1)].rearrange("p (i w) -> p i w", i=2)
                            act.activation(pv_lo[:, n % 2, :, :], src[:, :, D + 1:2 * D + 1], ACT.Copy)\
                               .then_inc(pv_half, 1)
                        elif kind == "proj":
                            if c == SEGS - 1:
                                nxt = p + 1
                                proj(a, at + k0 + 1, AT_PAIRS + k0, gp + 1, slice(nxt, nxt + 1)
                                     if isinstance(nxt, int) else bass.ds(nxt, 1))
                                k0 += 1
                        elif kind == "max":
                            k0 += 1
                        elif kind == "mt":
                            max_rows(a, at + k0 + 1, AT_PAIRS + k0, gp + 1)
                            k0 += 1
                        elif kind == "ot":
                            t0, m = OT_TILES[a]
                            until(act, work_full, at + k0 + 1)
                            cp = slice(p, p + 1) if isinstance(p, int) else bass.ds(p, 1)
                            act.activation(OT[:, 0, p, t0 * T:(t0 + m) * T],
                                           WK[(W_PRO + AT_PAIRS + k0) % 3][:, 0:m * T], ACT.Identity,
                                           bias=bias[:, 2, cp]).then_inc(work_hi, 1)
                            k0 += 1

                with act.Fori(0, PAIRS // 2 - 1) as j:
                    for r in range(2):
                        pair(2 * j + r, r, True)
                pair(PAIRS - 2, 0, True)
                pair(PAIRS - 1, 1, False)

        HI_PRO = 64
        HI_X, HI_V, HI_NEXT = 2 * NT, 2 * NT, 6
        HI_PAIR = HI_NEXT + 3
        HI_BATCH = HI_X + HI_V + HI_NEXT + (PAIRS - 1) * HI_PAIR + 3

        @block.vector
        def _(v):
            me = Chain(v, dve)

            def quantise_dve(k, src, scale_ap, y, m, q):
                me.step(v.tensor_scalar(y, src, scale_ap, None, ALU.mult))
                me.step(v.tensor_scalar(m.bitcast(u32), y.bitcast(u32), 0x7F800000, None, ALU.bitwise_and))
                v.tensor_scalar(m, m, 2.0 ** -6, 1.5 * 2.0 ** 20, ALU.max, ALU.mult).then_inc(q_m, 1)
                v.wait_ge(q_q, k)
                v.tensor_scalar(y, q, 2.0 ** 119 * 1.125, 0.0, ALU.mult, ALU.mult).then_inc(q_z, 1)

            v.memset(m_part[:, :, :, :], NEG)
            v.sem_inc(work_free, 3)
            v.sem_inc(st_free, 3)
            v.sem_inc(st_full, 1)
            v.sem_inc(w2_st, 16)
            for i in range(2):
                v.sem_inc(out_st[i], 16)
                v.sem_inc(y_st[i], 16)
            v.sem_inc(pv_full, 4)
            v.sem_inc(pv_free, 2)
            v.sem_inc(stage_dma[0], 96)
            v.sem_inc(stage_dma[1], 96)
            v.sem_inc(m_dma[0], 32)
            v.sem_inc(m_dma[1], 32)

            rmx = s_("rmx", 8)
            mx = s_("mx", 7)
            for g in range(4):
                v.wait_ge(raw_dma[g], 16 * NT)
                for i in range(NT):
                    ins = v.tensor_reduce(rmx[:, i:i + 1], raw[8 * g + i], AX.X, ALU.max,
                                          apply_absolute_value=True)
                me.step(ins)
                me.step(v.tensor_reduce(mx[:, g:g + 1], rmx, AX.X, ALU.max))
            v.wait_ge(work_full, 1)
            me.step(v.tensor_copy(bias[:, :, :].rearrange("p a n -> p (a n)"), WK[0][:, 0:24]))
            v.tensor_reduce(mx[:, 4:6], bias[:, 0:2, :], AX.X, ALU.max, apply_absolute_value=True)\
             .then_inc(work_free, 1)
            v.tensor_reduce(mx[:, 6:7], bias[:, 2, :], AX.X, ALU.max, apply_absolute_value=True)\
             .then_inc(mx_ready, 1)
            v.wait_ge(gmax, 1)
            g = s_("g", 7)
            bd, eb, ew, e1, e2 = s_("bd", 3), s_("eb", 3), s_("ew", 4), s_("e1", 1), s_("e2", 1)
            me.step(v.tensor_scalar(g, g, 2.0 ** -100, 2.0 ** 100, ALU.max, ALU.min))
            me.step(v.tensor_scalar(g[:, 0:2], g[:, 0:2], 2.0 ** -20, None, ALU.max))
            me.step(v.scalar_tensor_tensor(out=bd, in0=g[:, 0:3], scalar=1024.0, in1=g[:, 4:7],
                                           op0=ALU.mult, op1=ALU.add))
            me.step(v.tensor_scalar(eb.bitcast(u32), bd.bitcast(u32), 0x7F800000, None, ALU.bitwise_and))
            me.step(v.tensor_scalar(ew.bitcast(u32), g[:, 0:4].bitcast(u32), 0x7F800000, None, ALU.bitwise_and))

            def power(dst, src, e):
                return v.tensor_scalar(dst.bitcast(u32), src.bitcast(u32), -1.0, float((254 + e) << 23),
                                       ALU.mult, ALU.add)
            ss = s_("ss", 3)
            me.step(power(s_("w_s", 4), ew, 13))
            me.step(power(ss[:, 0:2], eb[:, 0:2], 11))
            me.step(power(ss[:, 2:3], eb[:, 2:3], 14))
            me.step(v.tensor_scalar(ew, ew, 2.0 ** -23, None, ALU.mult))
            for i, nm in enumerate(("c_q", "c_k", "c_v")):
                me.step(v.tensor_tensor(s_(nm), ss[:, i:i + 1], ew[:, i:i + 1], ALU.mult))
                me.step(v.tensor_scalar(bias[:, i, :], bias[:, i, :], ss[:, i:i + 1], None, ALU.mult))
            me.step(v.tensor_scalar(e1, eb[:, 0:1], 2.0 ** -11, None, ALU.mult))
            me.step(v.scalar_tensor_tensor(out=s_("e_s"), in0=eb[:, 1:2], scalar=2.0 ** -11 * D ** -0.5,
                                           in1=e1, op0=ALU.mult, op1=ALU.mult))
            me.step(v.tensor_scalar(e2, eb[:, 2:3], 2.0 ** -14 * 2.0 ** 10, None, ALU.mult))
            me.step(v.tensor_tensor(s_("c_o"), e2, ew[:, 3:4], ALU.mult))
            v.wait_ge(misc_dma, 48)
            me.step(v.reciprocal(e1, s_("scale")))
            me.step(v.reciprocal(e2, s_("scale1")))
            me.step(v.tensor_tensor(s_("c_f"), e1, e2, ALU.mult))
            me.n_pro = me.n
            v.tensor_scalar(s_("scale_x"), s_("scale"), 2.0 ** -10, None, ALU.mult).then_inc(sc_ready, 1)

            with v.Fori(0, NT) as t:
                me.base, me.n = me.n_pro + t * 2, 0
                v.wait_ge(w2_dma, (t + 1) * 16)
                quantise_dve(t + 1, w2t[0], s_("scale1"), w2y, w2m, w2q32)

            order = [(3, i) for i in range(8)]
            for p in range(PAIRS):
                order += [(0, p), (1, p), (2, p)]
            for i, (m, p) in enumerate(order):
                for g2 in range(2):
                    n = 1 + 2 * i + g2
                    src = WK[n % 3][:, :].rearrange("p (k f) -> p k f", k=4)
                    if m == 3:
                        hi, lo = (WO[:, l, 4 * g2:4 * g2 + 4, p * T:(p + 1) * T] for l in range(2))
                    elif m == 2:
                        hi, lo = (wv_stage[:, p % 4, l, 4 * g2:4 * g2 + 4, :] for l in range(2))
                    else:
                        hi, lo = (wqk[:, p % 2, m, l, 4 * g2:4 * g2 + 4, :] for l in range(2))
                    v.wait_ge(work_hi, n)
                    v.scalar_tensor_tensor(out=lo, in0=src, scalar=s_("w_s", 4)[:, m:m + 1], in1=hi,
                                           op0=ALU.mult, op1=ALU.subtract).then_inc(work_free, 1)
            stats = s_("stats", 12)
            v.memset(V[:, :, :, D:D + 1], 1.0)
            for r in range(2):
                for h in range(2):
                    v.memset(KB[r][h][D:D + 2, :], SHIFT)
            n0 = me.n_pro + 2 * NT
            PER_X = 5
            with v.Fori(0, B) as b:
                base = b * W_BATCH + W_PRO
                hb = b * HI_BATCH + HI_PRO
                me.base, me.n = n0 + b * (NT * PER_X), 0
                for t in range(NT):
                    a = xt[t % 2]
                    v.wait_ge(x_dma[t % 2], b * 64 + 16 * (t // 2 + 1))
                    v.bn_stats(stats[:, 0:6], a[:, 0:CH])
                    me.step(v.bn_stats(stats[:, 6:12], a[:, CH:H]))
                    v.sem_inc(held, 1)
                    me.step(v.bn_aggr(s_("mv", 2), stats))
                    v.tensor_scalar(s_("var"), s_("mv", 2)[:, 1:2], 1e-5, None, ALU.add).then_inc(var_ready, 1)
                    v.wait_ge(rstd_ready, b * NT + t + 1)
                    me.step(v.tensor_scalar(s_("rstd"), s_("rstd"), 2.0 ** 10, None, ALU.mult))
                    ins = v.tensor_scalar(a, a, s_("mv", 2)[:, 0:1], s_("rstd"), ALU.subtract, ALU.mult)
                    ins.then_inc(xn_ready, 1)
                    v.wait_ge(xn_ready, b * NT + t + 1)
                    quantise_dve(NT + b * NT + t + 1, a, s_("scale_x"), qy, qm, qq)
                    for g2 in range(2):
                        n = W_PRO + 3 * t + g2
                        v.wait_ge(work_hi, hb + 2 * t + g2 + 1)
                        hi, lo = (xs[:, l, 4 * g2:4 * g2 + 4, t * T:(t + 1) * T] for l in range(2))
                        v.tensor_tensor(lo, WK[n % 3][:, :].rearrange("p (k f) -> p k f", k=4), hi,
                                        ALU.subtract).then_inc(work_free, 1)
                    n = W_PRO + 3 * t + 2
                    v.wait_ge(work_full, base + 3 * t + 3)
                    v.tensor_copy(xq[:, :, t * T:(t + 1) * T],
                                  WK[n % 3][:, :].bitcast(bf16).rearrange("p (k f) -> p k f", k=NT))\
                     .then_inc(work_free, 1)
                for t in range(NT):
                    v.wait_ge(xb_ready, b * NT + t + 1)
                    for half in range(2):
                        k0 = AT_F + 2 * t + half
                        v.wait_ge(work_full, base + k0 + 1)
                        v.wait_ge(y_st[half], 16 + (b * NT + t) * 16)
                        v.scalar_tensor_tensor(out=yst[half], in0=WK[(W_PRO + k0) % 3][:, :],
                                               scalar=s_("c_f"), in1=xt[t % 2][:, half * CH:(half + 1) * CH],
                                               op0=ALU.mult, op1=ALU.add).then_inc(work_free, 1)
                for t in range(NT):
                    for half in range(2):
                        k0 = AT_V + 2 * t + half
                        v.wait_ge(work_hi, hb + HI_X + 2 * t + half + 1)
                        hi = V[:, t, 8 * half:8 * half + 8, 0:D]
                        lo = V[:, t, 8 * half:8 * half + 8, D + 1:2 * D + 1]
                        v.scalar_tensor_tensor(out=lo, in0=WK[(W_PRO + k0) % 3][:, :]
                                               .rearrange("p (h d) -> p h d", d=D), scalar=s_("c_v"), in1=hi,
                                               op0=ALU.mult, op1=ALU.subtract).then_inc(work_free, 1)

                def proj(n, k0, hi_n):
                    v.wait_ge(work_hi, hi_n)
                    v.tensor_tensor(stage[:, n % 2, 1, :], WK[(W_PRO + k0) % 3][:, :], stage[:, n % 2, 0, :],
                                    ALU.subtract).then_inc(work_free, 1)

                def maxima(h, u, k0, full):
                    v.wait_ge(work_full, full)
                    off = 0
                    for qt, k, w in MAX_UNITS[u]:
                        ins = v.tensor_reduce(m_part[:, h, qt, k // CH:k // CH + 1],
                                              WK[(W_PRO + k0) % 3][:, off:off + w], AX.X, ALU.max)
                        off += w
                    ins.then_inc(work_free, 1)
                    if u == NU - 1:
                        v.wait_ge(work_free, full + 3)
                        v.tensor_reduce(m_neg[:, h, :], m_part[:, h, :, :], AX.X, ALU.max,
                                        negate=True).then_inc(m_ready, 1)

                def max_rows(h, k0, hi_n):
                    v.wait_ge(work_hi, hi_n)
                    v.scalar_tensor_tensor(out=m_hl[:, h, 1, :], in0=WK[(W_PRO + k0) % 3][0:NT, 0:T],
                                           scalar=1.0 / SHIFT, in1=m_hl[:, h, 0, :],
                                           op0=ALU.mult, op1=ALU.subtract).then_inc(work_free, 1)

                at = base + AT_P0
                h0 = hb + HI_X + HI_V
                for n in range(4):
                    proj(n, AT_P0 + n, h0 + n + 1)
                for h in range(2):
                    for u in range(NU):
                        k0 = 4 + h * (NU + 1) + u
                        maxima(h, u, AT_P0 + k0, at + k0 + 1)
                    max_rows(h, AT_P0 + 4 + h * (NU + 1) + NU, h0 + 4 + h + 1)

                def pair(p, r, with_next):
                    at = base + AT_PAIRS + p * U_PAIR
                    hn = h0 + HI_NEXT + p * HI_PAIR
                    gp = b * PAIRS + p
                    k0 = his = 0
                    for kind, a, c in pair_steps(with_next):
                        if kind == "st":
                            n = a * NU + c
                            v.wait_ge(st_exp, gp * 2 * NU + n + 1)
                            v.tensor_tensor(P[:, c, 1, :], ST[n % 3][:, :], P[:, c, 0, :],
                                            ALU.subtract).then_inc(st_free, 1)
                        elif kind == "pv":
                            n = a * 4 + c
                            src = PV[n % 2][:, 0:2 * (2 * D + 1)].rearrange("p (i w) -> p i w", i=2)
                            v.wait_ge(o_done, gp * 8 + n + 1)
                            v.wait_ge(pv_half, gp * 8 + n + 1)
                            v.reciprocal(pv_rec[:, n % 2, :, :], src[:, :, D:D + 1])
                            v.tensor_tensor(pv_num[:, n % 2, :, :], src[:, :, 0:D], pv_lo[:, n % 2, :, :],
                                            ALU.add).then_inc(pv_free, 1)
                        elif kind == "proj":
                            if c == SEGS - 1:
                                his += 1
                                proj(a, AT_PAIRS + k0, hn + his)
                                k0 += 1
                        elif kind == "max":
                            maxima(a, c, AT_PAIRS + k0, at + k0 + 1)
                            k0 += 1
                        elif kind == "mt":
                            his += 1
                            max_rows(a, AT_PAIRS + k0, hn + his)
                            k0 += 1
                        elif kind == "ot":
                            his += 1
                            t0, m = OT_TILES[a]
                            v.wait_ge(work_hi, hn + his)
                            cp = slice(p, p + 1) if isinstance(p, int) else bass.ds(p, 1)
                            v.scalar_tensor_tensor(out=OT[:, 1, p, t0 * T:(t0 + m) * T],
                                                   in0=WK[(W_PRO + AT_PAIRS + k0) % 3][:, 0:m * T],
                                                   scalar=bias[:, 2, cp], in1=OT[:, 0, p, t0 * T:(t0 + m) * T],
                                                   op0=ALU.add, op1=ALU.subtract).then_inc(work_free, 1)
                            k0 += 1

                with v.Fori(0, PAIRS // 2 - 1) as j:
                    for r in range(2):
                        pair(2 * j + r, r, True)
                pair(PAIRS - 2, 0, True)
                pair(PAIRS - 1, 1, False)

                for t in range(NT):
                    for half in range(2):
                        k0 = AT_OUT + 2 * t + half
                        v.wait_ge(work_full, base + k0 + 1)
                        v.wait_ge(y_dma[t % 2], b * 64 + 16 * (t // 2 + 1))
                        y = xt[t % 2][:, half * CH:(half + 1) * CH]
                        v.scalar_tensor_tensor(out=y, in0=WK[(W_PRO + k0) % 3][:, :], scalar=s_("c_o"),
                                               in1=y, op0=ALU.mult, op1=ALU.add).then_inc(work_free, 1)

        @block.gpsimd
        def _(g):
            me = Chain(g, pool)
            g.sem_inc(o_done, 2)
            g.memset(s_("half"), -0.5).then_inc(consts, 1)
            me.step(g.memset(ident[:, :], 0.0))
            g.affine_select(out=ident[:, :], in_=ident[:, :], compare_op=ALU.not_equal, fill=1.0, base=0,
                            pattern=[[-1, T]], channel_multiplier=1).then_inc(consts, 1)
            me.step(g.memset(identb[:, :], 0.0))
            g.affine_select(out=identb[:, :], in_=identb[:, :], compare_op=ALU.not_equal, fill=1.0, base=0,
                            pattern=[[-1, T]], channel_multiplier=1).then_inc(consts, 1)
            me.step(g.memset(maskb[:, :], 0.0))
            g.affine_select(out=maskb[:, :], in_=maskb[:, :], compare_op=ALU.is_ge, fill=NEG, base=0,
                            pattern=[[-1, T]], channel_multiplier=1).then_inc(consts, 2)
            g.wait_ge(mx_ready, 1)
            g.partition_all_reduce(s_("g", 7), s_("mx", 7), T, bass.bass_isa.ReduceOp.max).then_inc(gmax, 1)

            def quantise_pool(k, y, m, q, dst):
                g.wait_ge(q_m, k)
                me.step(g.tensor_tensor(y, y, m, ALU.add))
                g.tensor_tensor(q, y, m, ALU.subtract).then_inc(q_q, 1)
                g.wait_ge(q_z, k)
                g.tensor_tensor(dst, q, y, ALU.add).then_inc(q_done, 1)

            n_pro = me.n
            with g.Fori(0, NT) as t:
                me.base, me.n = n_pro + t, 0
                g.wait_ge(w2_st, 16 + t * 16)
                quantise_pool(t + 1, w2y, w2m, w2q32, w2b[0])

            with g.Fori(0, B) as b:
                base = b * W_BATCH + W_PRO
                me.base, me.n = n_pro + NT + b * NT, 0
                for t in range(NT):
                    g.wait_ge(var_ready, b * NT + t + 1)
                    g.tensor_tensor(s_("rstd"), s_("var"), s_("half"), ALU.pow).then_inc(rstd_ready, 1)
                    g.wait_ge(work_full, base + 3 * t)
                    quantise_pool(NT + b * NT + t + 1, qy, qm, qq, xqt)
                g.wait_ge(bout_dma, (b + 1) * 16)
                for t in range(NT):
                    g.wait_ge(xf_dma[t % 2], b * 64 + 16 * (t // 2 + 1))
                    g.tensor_tensor(xt[t % 2], xt[t % 2], bout, ALU.add).then_inc(xb_ready, 1)

                def pair(p, r, with_next):
                    gp = b * PAIRS + p
                    for kind, a, c in pair_steps(with_next):
                        if kind == "pv":
                            n = a * 4 + c
                            g.wait_ge(pv_free, 2 + gp * 8 + n + 1)
                            if n == 0:
                                g.wait_ge(work_full, base + AT_PAIRS + p * U_PAIR)
                            dst = ost[:, 2 * c:2 * c + 2, a * D:(a + 1) * D]
                            g.tensor_tensor(dst, pv_num[:, n % 2, :, :],
                                            pv_rec[:, n % 2, :, :].to_broadcast((T, 2, D)),
                                            ALU.mult).then_inc(o_done, 1)

                with g.Fori(0, PAIRS // 2 - 1) as j:
                    for r in range(2):
                        pair(2 * j + r, r, True)
                pair(PAIRS - 2, 0, True)
                pair(PAIRS - 1, 1, False)


_INS = ['L0_attn_x', 'L0_attn_W_qkv', 'L0_attn_b_qkv', 'L0_attn_W_out', 'L0_attn_b_out',
        'L0_ffn_input2', 'L0_ffn_scale', 'L0_ffn_scale1']
_OUTS = [((B, S, H), 'float32')]


def kernel(**inputs):
    import numpy as _np
    import concourse.bacc as _bacc
    from concourse import mybir as _mybir
    from concourse.bass_utils import run_bass_kernel_spmd as _run

    nc = _bacc.Bacc("TRN2", target_bir_lowering=False, num_devices=1)
    arrays, args = {}, []
    for name in _INS:
        a = _np.ascontiguousarray(inputs[name])
        if a.ndim == 0:
            a = a.reshape(1, 1)
        arrays[f"in_{name}_dram"] = a
        args.append(nc.dram_tensor(f"in_{name}_dram", a.shape, _mybir.dt.from_np(a.dtype), kind="ExternalInput").ap())
    for i, (shape, dtype) in enumerate(_OUTS):
        dt = _mybir.dt.from_np(_np.dtype(dtype))
        args.append(nc.dram_tensor(f"out_{i}_dram", shape, dt, kind="ExternalOutput").ap())
    block_kernel(nc, *args)
    r = _run(nc, [arrays], core_ids=[0])
    got = tuple(r.results[0][f"out_{i}_dram"] for i in range(len(_OUTS)))
    return got[0]
```

```python
import concourse.bass as bass
from concourse import mybir
from contextlib import ExitStack

B, S, H = 4, 1024, 1024
HEADS, D = 16, 64
PAIRS = HEADS // 2
T = 128
NT = S // T
CH = 512
VW = 2 * D + 2

ST_UNITS = [
    [(0, 0, 512)],
    [(1, 128, 384), (3, 384, 128)],
    [(2, 256, 256), (6, 768, 256)],
    [(0, 512, 512)], [(1, 512, 512)], [(2, 512, 512)], [(3, 512, 512)],
    [(4, 512, 512)],
    [(5, 640, 384), (7, 896, 128)],
]
MAX_UNITS = [
    [(0, 0, 128), (2, 0, 384)],
    [(3, 0, 512)],
    [(4, 0, 512)],
    [(5, 0, 512)],
    [(6, 0, 512)],
    [(7, 0, 512)],
    [(1, 0, 256), (5, 512, 256)],
    [(4, 512, 128), (6, 512, 384)],
    [(7, 512, 512)],
]
PROJ_UNITS = [(1, 0), (0, 0), (0, 1), (1, 1)]
MAX_NEEDS = {0: [(0, 64), (1, 64)], 2: [(0, 128)], 6: [(1, 128)]}
NU = len(ST_UNITS)
SEGS = 4


def block_at(kb, qt):
    for u, parts in enumerate(ST_UNITS):
        off = 0
        for k, q0, w in parts:
            if k == kb and q0 <= qt * T < q0 + w:
                return u, off + qt * T - q0
            off += w
    raise ValueError((kb, qt))


PAIR_ORDER = """
    proj x now proj now proj now proj now st st proj now st now proj st now st proj pv now st
    proj now st pv st proj now st proj proj now x proj x pv proj st proj st proj next proj pv st
    next st next st next pv st next next st st pv st xt xt next pv next next xt pv next ot ot ot
    ot next
""".split()
LAST_ORDER = """
    x now now x now now now x st now st now st now st now st pv st st now st now pv st xt xt xt
    pv st st st pv st st pv st st pv st st ot ot pv pv ot ot
""".split()


def pair_steps(with_next, with_x):
    rows = {
        "st": [("st", h, u) for h in range(2) for u in range(NU)],
        "pv": [("pv", h, c) for h in range(2) for c in range(4)],
        "ot": [("ot", t, 0) for t in range(0, NT, 2)],
        "proj": [("proj", n, s) for n in range(4) for s in range(SEGS)],
        "now": [("max", 1, u) for u in range(NU)] + [("mt", 1, 0), ("mr", 1, 0)],
        "next": [("max", 2, u) for u in range(NU)] + [("mt", 2, 0), ("mr", 2, 0)],
        "x": [("xs", 0, 0), ("xn", 0, 0), ("xm", 0, 0)],
        "xt": [("xf", 0, 0), ("xf", 1, 0), ("xb", 0, 0)],
    }
    order = PAIR_ORDER if with_next else LAST_ORDER
    return [rows[word].pop(0) for word in order if with_x or word not in ("x", "xt")]


def first_steps():
    out = [("ffn", t, half) for t in range(NT) for half in range(2)]
    v = [("v", t, half) for t in range(NT) for half in range(2)]
    out += v[:2]
    v = v[2:]
    for n in range(4):
        out += [("proj", n, s) for s in range(SEGS)] + [v.pop(0)]
    mx = [("max", 2, u) for u in range(NU)] + [("mt", 2, 0)]
    while v or mx:
        if v:
            out.append(v.pop(0))
        if mx:
            out.append(mx.pop(0))
    return out + [("mr", 2, 0)]


def is_unit(step):
    kind = step[0]
    return kind in ("max", "mt", "ot", "xf", "xb", "ffn", "v")


def has_hi(step):
    return is_unit(step) and step[0] not in ("max", "xb", "ffn")


def units(steps):
    return sum(map(is_unit, steps))


def his(steps):
    return sum(map(has_hi, steps))


W_ORDER = [NT * m + i for m in (0, 2, 3, 1) for i in range(NT)]

W2_EVERY = 3

W_PRO, HI_PRO = 1 + 3 * NT + 2 * len(W_ORDER), 2 * NT + 2 * len(W_ORDER)


class Count:

    def __init__(self, f, out_units, with_x):
        self.first = f(first_steps())
        self.pair = f(pair_steps(True, with_x))
        self.last = f(pair_steps(False, with_x))
        self.at_out = self.first + (PAIRS - 1) * self.pair + self.last
        self.all = self.at_out + out_units


U = [Count(units, 2 * NT, x) for x in (False, True)]
HI = [Count(his, 0, x) for x in (False, True)]
assert U[0].pair % 3 == 0 and U[1].pair % 3 == 0 and U[1].all % 3 == 0

SHIFT = 32768.0
NEG = -1.0e30


def block_kernel(nc, x, w_qkv, b_qkv, w_out, b_out, w2, scale, scale1, out):
    fp32, f16, bf16 = mybir.dt.float32, mybir.dt.float16, mybir.dt.bfloat16
    u32 = mybir.dt.uint32
    ALU = mybir.AluOpType
    ACT = mybir.ActivationFunctionType
    AX = mybir.AxisListType

    w_d = nc.dram_tensor("w_split", (4 * NT, T, 2 * NT * T), f16, kind="Internal").ap()
    w2_d = nc.dram_tensor("w2_quantised", (NT, T, H), bf16, kind="Internal").ap()
    xs_d = nc.dram_tensor("x_split", (B * NT, T, 2 * NT * T), f16, kind="Internal").ap()
    xq_d = nc.dram_tensor("x_quantised", (B * NT, T, NT * T), bf16, kind="Internal").ap()
    y_d = nc.dram_tensor("ffn_part", (B * NT, T, H), fp32, kind="Internal").ap()
    x_t = x.rearrange("b (t p) h -> (b t) p h", p=T)
    out_t = out.rearrange("b (t p) h -> (b t) p h", p=T)

    ctx = ExitStack()
    with ctx:
        def sem(name):
            return ctx.enter_context(nc.semaphore(name))

        def small(name, shape, dt):
            return ctx.enter_context(nc.sbuf_tensor(name, shape, dt))

        xs_r = small("xs_region", [T, 8192], fp32)
        v_r = small("v_region", [T, NT * HEADS * VW // 2], fp32)
        w_r = small("wqk_region", [T, 4096], fp32)
        s_r = small("stack_region", [T, 8192], fp32)
        p_r = small("p_region", [T, NU * CH], fp32)
        o_r = small("ot_region", [T, 8192], fp32)
        wo_r = small("wo_region", [T, 8192], fp32)
        ost = small("o_rows", [T, NT, T], fp32)
        stage = small("qk_stage", [T, 2, 2, CH], f16)
        m_hl = small("max_rows", [NT, 2, 2, T], f16)
        ident = small("ident", [T, T], fp32)
        identb = small("identb", [T, T], bf16)
        maskb = small("mask_future", [T, T], bf16)
        pv_lo = small("pv_lo", [T, 2, 2, D], fp32)
        pv_num = small("pv_num", [T, 2, 2, D], fp32)
        pv_rec = small("pv_rec", [T, 2, 2, 1], fp32)
        m_part = small("max_parts", [T, 2, NT, 2], fp32)
        m_neg = small("max_negated", [T, 2, NT], fp32)
        bias = small("biases", [T, 3, NT], fp32)
        sc = small("scalars", [T, 104], fp32)

        def tiles16(region, dt=f16):
            return region.bitcast(dt).rearrange("p (g l k f) -> p g l k f", l=2, k=NT, f=T)

        xs = tiles16(xs_r[:, :])
        WV = tiles16(o_r[:, :])
        WO = tiles16(wo_r[:, :])
        wqk = tiles16(w_r[:, :])
        V = v_r[:, :].bitcast(f16).rearrange("p (t h w) -> p t h w", t=NT, h=HEADS)
        w2q = w_r[:, :].bitcast(bf16).rearrange("p (k n) -> p k n", k=NT)
        P = p_r[:, :].bitcast(f16).rearrange("p (u l q) -> p u l q", u=NU, l=2)
        xq = p_r[:, 0:4096].bitcast(bf16).rearrange("p (t k f) -> p t k f", t=NT, k=NT)
        OT = o_r[:, :].bitcast(f16).rearrange("p (l g t) -> p l g t", l=2, g=PAIRS)

        stk = s_r[:, :].bitcast(f16).rearrange("p (r w t) -> p r w t", r=2, w=8)
        QA = [[stk[:, r, 2 * h, :] for h in range(2)] for r in range(2)]
        QB = [[stk[:, r, 2 * h + 1, :] for h in range(2)] for r in range(2)]
        KA = [[stk[:, r, 4 + h, :] for h in range(2)] for r in range(2)]
        KB = [[stk[:, r, 6 + h, :] for h in range(2)] for r in range(2)]

        xr = [s_r[:, 1024 * i:1024 * i + 1024] for i in range(3)]
        bout = ost[:, :, :].rearrange("p a f -> p (a f)")
        yt = [s_r[:, 4096 + 1024 * i:5120 + 1024 * i] for i in range(2)]
        yst = [[s_r[:, 6144:6656], s_r[:, 6656:7168]], [wo_r[:, 4096:4608], wo_r[:, 4608:5120]]]

        xt = [wo_r[:, 1024 * i:1024 * i + 1024] for i in range(2)]
        qy, qm, qq = (wo_r[:, 2048 + 1024 * i:3072 + 1024 * i] for i in range(3))
        xqt = wo_r[:, 5120:5632].bitcast(bf16)
        xst = tiles16(wo_r[:, 5632:6656])[:, 0]
        xqs = wo_r[:, 6656:7168].bitcast(bf16)
        qk32 = [wo_r[:, 7168 + CH * i:7168 + CH * (i + 1)] for i in range(2)]

        raw = [reg[:, 1024 * i:1024 * i + 1024] for reg in (xs_r, v_r, s_r, o_r) for i in range(NT)]
        w2t, w2q32 = (w_r[:, 1024 * i:1024 * i + 1024] for i in range(2))
        w2y = [w_r[:, 2048:3072], wo_r[:, 7168:8192]]
        w2m = [w_r[:, 3072:4096], wo_r[:, 4096:5120]]
        w2b = p_r[:, 4096:4608].bitcast(bf16)
        wst = tiles16(wo_r[:, 0:4096])

        col = {}

        def s_(name, n=1):
            if name not in col:
                col[name] = (sum(w for _, w in col.values()), n)
            a, w = col[name]
            return sc[:, a:a + w]

        WK = [ctx.enter_context(nc.psum_tensor(f"work{i}", [T, CH], fp32)) for i in range(3)]
        ST = [ctx.enter_context(nc.psum_tensor(f"scores{i}", [T, CH], fp32)) for i in range(3)]
        PV = ctx.enter_context(nc.psum_tensor("pv", [T, CH], fp32))
        PJ = ctx.enter_context(nc.psum_tensor("proj", [T, CH], fp32))

        work_full = sem("work_full")
        work_hi = sem("work_hi")
        work_free = sem("work_free")
        st_full = sem("st_full")
        st_exp = sem("st_exp")
        st_free = sem("st_free")
        pv_full = sem("pv_full")
        pv_half = sem("pv_half")
        pv_free = sem("pv_free")
        pj_full = sem("pj_full")
        pj_free = sem("pj_free")
        pj_hi = sem("pj_hi")
        pj_lo = sem("pj_lo")
        o_done = sem("o_done")
        m_ready = sem("m_ready")
        stage_dma = [sem(f"stage_dma{i}") for i in range(2)]
        m_dma = [sem(f"m_dma{i}") for i in range(2)]
        w_dma = [sem(f"w_dma{i}") for i in range(2)]
        x_dma = [sem(f"x_dma{i}") for i in range(2)]
        xr_dma = [sem(f"xr_dma{i}") for i in range(3)]
        y_dma = [sem(f"y_dma{i}") for i in range(2)]
        y_st = [[sem(f"y_st{i}{h}") for h in range(2)] for i in range(2)]
        out_st = [sem(f"out_st{i}") for i in range(2)]
        xs_st, xq_st = sem("xs_st"), sem("xq_st")
        xs_dma, xq_dma = sem("xs_dma"), sem("xq_dma")
        wv_dma, wo_dma, w2q_dma = sem("wv_dma"), sem("wo_dma"), sem("w2q_dma")
        bout_dma = sem("bout_dma")
        raw_dma = [sem(f"raw_dma{i}") for i in range(NT)]
        misc_dma = sem("misc_dma")
        w2_dma = sem("w2_dma")
        w2_st = sem("w2_st")
        w_st = [sem(f"w_st{i}") for i in range(4)]
        consts = sem("consts")
        gmax = sem("gmax")
        mx_ready = sem("mx_ready")
        sc_ready = sem("sc_ready")
        dve = sem("dve")
        pool = sem("pool")
        var_ready, rstd_ready = sem("var_ready"), sem("rstd_ready")
        xn_ready = sem("xn_ready")
        q_y, q_m, q_done = sem("q_y"), sem("q_m"), sem("q_done")
        w2_y, w2_m, w2_done = sem("w2_y"), sem("w2_m"), sem("w2_done")
        xb_ready = sem("xb_ready")
        held = sem("held")

        class Chain:

            def __init__(self, eng, s):
                self.eng, self.s, self.base, self.n = eng, s, 0, 0

            def step(self, ins):
                ins.then_inc(self.s, 1)
                self.n += 1
                self.eng.wait_ge(self.s, self.base + self.n)

        def until(eng, s, value):
            eng.wait_ge(s, value)
            eng.sem_inc(held, 1)

        def at(i):
            return slice(i, i + 1) if isinstance(i, int) else bass.ds(i, 1)

        def batches(eng, body):
            with eng.Fori(0, B - 1) as b:
                body(b, True)
            body(B - 1, False)

        def pairs(eng, body):
            with eng.Fori(0, PAIRS // 2 - 1) as j:
                for r in range(2):
                    body(2 * j + r, r, j, True, True)
            body(PAIRS - 2, 0, PAIRS // 2 - 1, True, False)
            body(PAIRS - 1, 1, PAIRS // 2 - 1, False, False)

        block = ctx.enter_context(nc.Block())

        @block.sync
        def _(sp):
            sp.dma_start(ost[0:24, 0, :], b_qkv.rearrange("(a p) -> a p", p=T)).then_inc(misc_dma, 16)
            sp.dma_start(s_("scale"), scale.to_broadcast((T, 1))).then_inc(misc_dma, 16)
            sp.dma_start(s_("scale1"), scale1.to_broadcast((T, 1))).then_inc(misc_dma, 16)

            def load_x(k, slot):
                sp.dma_start(xt[slot], x_t[k, :, :]).then_inc(x_dma[slot], 16)

            def store_x(k, free):
                until(sp, work_free, free)
                sp.dma_start(xs_d[k, :, :], wo_r[:, 5632:6656].bitcast(f16)).then_inc(xs_st, 16)
                sp.dma_start(xq_d[k, :, :], xqs).then_inc(xq_st, 16)

            def load_raw(i):
                for g, src in enumerate((w_qkv[0:H, :], w_qkv[H:2 * H, :], w_qkv[2 * H:3 * H, :], w_out)):
                    sp.dma_start(raw[NT * g + i], src[i * T:(i + 1) * T, :]).then_inc(raw_dma[i], 16)

            load_x(0, 0)
            load_x(1, 1)
            load_raw(0)
            load_raw(1)
            for t in range(NT):
                if t == 0:
                    sp.dma_start(w2t, w2[0:T, :]).then_inc(w2_dma, 16)
                if t + 2 < NT:
                    sp.wait_ge(work_full, 1 + 3 * t + 2)
                    sp.wait_ge(q_y, t + 1)
                    load_x(t + 2, t % 2)
                    load_raw(t + 2)
                store_x(t, 3 + 1 + 3 * (t + 1))
            def load_batch(b):
                until(sp, xs_st, (b + 1) * NT * 16)
                until(sp, xq_st, (b + 1) * NT * 16)
                sp.dma_start(xs_r[:, :].bitcast(f16).rearrange("p (t n) -> p t n", t=NT),
                             xs_d[bass.ds(b * NT, NT), :, :].rearrange("t p n -> p t n")).then_inc(xs_dma, 16)

            def load_quantised(b):
                sp.dma_start(p_r[:, 0:4096].bitcast(bf16).rearrange("p (t n) -> p t n", t=NT),
                             xq_d[bass.ds(b * NT, NT), :, :].rearrange("t p n -> p t n")).then_inc(xq_dma, 16)

            def load_w2():
                sp.dma_start(w2q, w2_d.rearrange("k p n -> p k n")).then_inc(w2q_dma, 16)

            def load_b_out():
                sp.dma_start(bout, b_out.rearrange("(a n) -> a n", a=1).to_broadcast((T, H)))\
                  .then_inc(bout_dma, 16)

            def load_xr(b):
                for t in range(3):
                    sp.dma_start(xr[t], x_t[b * NT + t, :, :]).then_inc(xr_dma[t], 16)

            def load_pair(p, slot):
                for i in range(2):
                    sp.dma_start(w_r[:, 2048 * slot + 1024 * i:2048 * slot + 1024 * i + 1024].bitcast(f16),
                                 w_d[p + NT * i, :, :]).then_inc(w_dma[slot], 16)

            def stacks(n, r, gp):
                kind, half = PROJ_UNITS[n]
                s, c = n % 2, slice(half * CH, half * CH + CH)
                until(sp, pj_lo, 2 + gp * 4 + n + 1)
                for h in range(2):
                    rows = slice(D * h, D * h + D)
                    hi, lo = stage[rows, s, 0, :], stage[rows, s, 1, :]
                    if kind == 0:
                        todo = [(stk[0:D, r, 2 * h:2 * h + 2, c], stage[rows, s, :, :]), (QA[r][h][D:T, c], hi)]
                    else:
                        todo = [(stk[0:D, r, 4 + h:8:2, c], stage[rows, s, 0:1, :].to_broadcast((D, 2, CH))),
                                (KA[r][h][D:T, c], lo)]
                    for dst, src in todo:
                        sp.dma_start(dst, src).then_inc(stage_dma[s], 16)

            for i, w in enumerate(W_ORDER):
                t = i // W2_EVERY
                if i % W2_EVERY == 1 and 1 <= t <= NT:
                    sp.wait_ge(w2_done, t)
                    sp.dma_start(w2_d[t - 1, :, :], w2b).then_inc(w2_st, 16)
                if i % W2_EVERY == 2 and t < NT - 1:
                    sp.wait_ge(w2_y, t + 1)
                    sp.dma_start(w2t, w2[(t + 1) * T:(t + 2) * T, :]).then_inc(w2_dma, 16)
                sp.wait_ge(work_free, 3 + 1 + 3 * NT + 2 * (i + 1))
                sp.dma_start(w_d[w, :, :], wo_r[:, 1024 * (i % 4):1024 * (i % 4) + 1024].bitcast(f16))\
                  .then_inc(w_st[i % 4], 16)
                if i == W2_EVERY * NT + 2:
                    sp.wait_ge(w2_st, 16 * NT)
                    load_w2()
                    sp.wait_ge(xq_st, 16 * NT)
                    load_quantised(0)
                    load_b_out()
                    load_xr(0)
            for q in w_st:
                sp.wait_ge(q, 16 * len(W_ORDER) // 4)
            load_batch(0)

            def batch(b, with_x):
                n = U[with_x]
                base = b * U[1].all + W_PRO
                until(sp, work_full, base)
                wv_rows = o_r[:, :].bitcast(f16).rearrange("p (g n) -> p g n", g=NT)
                if with_x:
                    load_x((b + 1) * NT, 0)
                u = 0
                for step in first_steps():
                    kind, a, c = step
                    u += is_unit(step)
                    if kind == "ffn":
                        until(sp, work_free, base + 3 + u)
                        sp.dma_start(y_d[b * NT + a, :, c * CH:(c + 1) * CH], yst[a % 2][c])\
                          .then_inc(y_st[a % 2][c], 16)
                        if c == 1 and a + 3 < NT:
                            sp.dma_start(xr[a % 3], x_t[b * NT + a + 3, :, :]).then_inc(xr_dma[a % 3], 16)
                        if c == 1 and a < NT // 2:
                            sp.dma_start(wv_rows[:, 2 * a:2 * a + 2, :],
                                         w_d[2 * NT + 2 * a:2 * NT + 2 * a + 2, :, :].rearrange("g p n -> p g n"))\
                              .then_inc(wv_dma, 16)
                        if a == NT - 1 and c == 1:
                            load_pair(0, 0)
                            load_pair(1, 1)
                    elif kind == "proj" and c == SEGS - 1:
                        stacks(a, 0, b * PAIRS)
                for half in range(2):
                    for q in y_st[half]:
                        until(sp, q, 16 + (b + 1) * NT * 8)

                def pair(p, r, turn, with_next, more):
                    u = 0
                    if more:
                        load_pair(p + 2, r)
                    if with_x and with_next:
                        load_x((b + 1) * NT + p + 1, 1 - r)
                    if with_next:
                        until(sp, st_full, 1 + (b * PAIRS + p) * 2 * NU)
                    for step in pair_steps(with_next, with_x):
                        kind, a, c = step
                        u += is_unit(step)
                        k = base + 3 + n.first + p * n.pair + u
                        if kind == "proj" and c == SEGS - 1:
                            stacks(a, 1 - r, b * PAIRS + p + 1)
                        elif kind == "xb":
                            store_x((b + 1) * NT + p, k)
                            if not with_next:
                                load_w_out()
                                load_batch(b + 1)
                    if not with_next and not with_x:
                        load_w_out()

                def load_w_out():
                    sp.dma_start(wo_r[:, :].bitcast(f16).rearrange("p (g n) -> p g n", g=NT),
                                 w_d[3 * NT:4 * NT, :, :].rearrange("g p n -> p g n")).then_inc(wo_dma, 16)

                pairs(sp, pair)
                until(sp, st_full, 1 + (b + 1) * PAIRS * 2 * NU)
                for t in range(2):
                    sp.dma_start(yt[t], y_d[b * NT + t, :, :]).then_inc(y_dma[t], 16)
                if with_x:
                    until(sp, pv_full, 4 + (b + 1) * PAIRS * 8)
                    load_quantised(b + 1)
                    load_w2()
                    load_xr(b + 1)
                for t in range(NT):
                    until(sp, work_free, base + 3 + n.at_out + 2 * (t + 1))
                    if with_x and t == 0:
                        load_b_out()
                    sp.dma_start(out_t[b * NT + t, :, :], yt[t % 2]).then_inc(out_st[t % 2], 16)
                    if t + 2 < NT:
                        until(sp, out_st[t % 2], 16 + b * 64 + 16 * (t // 2 + 1))
                        sp.dma_start(yt[t % 2], y_d[b * NT + t + 2, :, :]).then_inc(y_dma[t % 2], 16)

            batches(sp, batch)
            for s in range(2):
                sp.wait_ge(out_st[s], 16 + B * 64)

        @block.tensor
        def _(pe):
            pe.wait_ge(consts, 5)
            pe.wait_ge(misc_dma, 48)
            pe.wait_ge(work_free, 1)
            pe.transpose(WK[0][:, 0:24], ost[0:24, 0, :], ident[0:24, 0:24]).then_inc(work_full, 1)

            def x_rows(g, slot, bank, k):
                pe.wait_ge(xn_ready, k + 1)
                for i in range(4):
                    ins = pe.transpose(bank[:, i * T:(i + 1) * T],
                                       xt[slot][:, (4 * g + i) * T:(4 * g + i + 1) * T], ident[:, :])
                ins.then_inc(work_full, 1)

            def x_quantised(bank, k):
                pe.wait_ge(q_done, k + 1)
                tb = bank[:, :].bitcast(bf16)
                for i in range(NT):
                    ins = pe.transpose(tb[:, i * T:(i + 1) * T], xqt[:, i * T:(i + 1) * T], identb[:, :])
                ins.then_inc(work_full, 1)

            for t in range(NT):
                for g in range(3):
                    n = 1 + 3 * t + g
                    pe.wait_ge(work_free, n + 1)
                    if g < 2:
                        x_rows(g, t % 2, WK[n % 3], t)
                    else:
                        x_quantised(WK[n % 3], t)
            for i, w in enumerate(W_ORDER):
                pe.wait_ge(raw_dma[w % NT], 64)
                for g in range(2):
                    n = 1 + 3 * NT + 2 * i + g
                    pe.wait_ge(work_free, n + 1)
                    for k in range(4):
                        ins = pe.transpose(WK[n % 3][:, k * T:(k + 1) * T],
                                           raw[w][:, (4 * g + k) * T:(4 * g + k + 1) * T], ident[:, :])
                    ins.then_inc(work_full, 1)

            def split_product(bank, n, stationary, moving, lo=0, hi=None):
                for k in range(lo, n if hi is None else hi):
                    for i, (a, b) in enumerate(((0, 0), (0, 1), (1, 0))):
                        ins = pe.matmul(bank[:, :], stationary(a, k), moving(b, k),
                                        start=(k == 0 and i == 0), stop=(k == n - 1 and i == 2))
                return ins

            def batch(b, with_x):
                nu = U[with_x]
                base = b * U[1].all + W_PRO

                def proj(n, seg, s, gp):
                    kind, c = PROJ_UNITS[n]
                    if seg == 0:
                        pe.wait_ge(pj_free, gp * 4 + n + 1)
                    ins = split_product(PJ, NT, lambda l, k: wqk[:, 2 * s + kind, l, k, :],
                                        lambda l, k: xs[:, 4 * c:4 * c + 4, l, k, :],
                                        seg * NT // SEGS, (seg + 1) * NT // SEGS)
                    if seg == SEGS - 1:
                        ins.then_inc(pj_full, 1)

                def maxima(h, u, r, bank, free):
                    pe.wait_ge(work_free, free)
                    off = 0
                    for qt, k, w in MAX_UNITS[u]:
                        ins = pe.matmul(bank[:, off:off + w], QA[r][h][:, qt * T:(qt + 1) * T],
                                        KA[r][h][:, k:k + w], start=True, stop=True)
                        if k <= qt * T < k + w:
                            d = off + qt * T - k
                            ins = pe.matmul(bank[:, d:d + T], identb[:, :], maskb[:, :],
                                            start=False, stop=True, skip_group_check=True)
                        off += w
                    ins.then_inc(work_full, 1)

                def max_transpose(h, bank, free, ready):
                    pe.wait_ge(work_free, free)
                    pe.wait_ge(m_ready, ready)
                    pe.transpose(bank[0:NT, 0:T], m_neg[:, h, :], ident[:, :]).then_inc(work_full, 1)

                u = 0
                for step in first_steps():
                    kind, a, c = step
                    bank = WK[(W_PRO + u) % 3]
                    free = base + u + 1
                    if kind == "ffn":
                        if a == 0 and c == 0:
                            pe.wait_ge(w2q_dma, (b + 1) * 16)
                            pe.wait_ge(xq_dma, (b + 1) * 16)
                        pe.wait_ge(work_free, free)
                        for k in range(NT):
                            ins = pe.matmul(bank[:, :], xq[:, a, k, :], w2q[:, k, c * CH:(c + 1) * CH],
                                            start=(k == 0), stop=(k == NT - 1))
                        ins.then_inc(work_full, 1)
                    elif kind == "v":
                        if a == 0 and c == 0:
                            pe.wait_ge(wv_dma, (b + 1) * 64)
                            pe.wait_ge(xs_dma, (b + 1) * 16)
                        pe.wait_ge(work_free, free)
                        split_product(bank, NT, lambda l, k: xs[:, a, l, k, :],
                                      lambda l, k: WV[:, 4 * c:4 * c + 4, l, k, :]).then_inc(work_full, 1)
                    elif kind == "proj":
                        if a == 0 and c == 0:
                            pe.wait_ge(w_dma[0], b * PAIRS * 16 + 32)
                        proj(a, c, 0, b * PAIRS)
                    elif kind == "max":
                        for s, count in MAX_NEEDS.get(c, []):
                            pe.wait_ge(stage_dma[s], 64 + b * PAIRS * 128 + count)
                        maxima(0, c, 0, bank, free)
                    elif kind == "mt":
                        max_transpose(0, bank, free, b * HEADS + 1)
                    u += is_unit(step)

                def pair(p, r, turn, with_next, more):
                    gp = b * PAIRS + p
                    u = 0
                    for step in pair_steps(with_next, with_x):
                        kind, a, c = step
                        bank = WK[(W_PRO + nu.first + u) % 3]
                        free = base + nu.first + p * nu.pair + u + 1
                        if kind == "st":
                            if c == 0:
                                pe.wait_ge(m_dma[a], 32 + (gp + 1) * 32)
                            n = a * NU + c
                            bank = ST[n % 3]
                            pe.wait_ge(st_free, gp * 2 * NU + n + 1)
                            off = 0
                            for kb, q0, w in ST_UNITS[c]:
                                pe.matmul(bank[:, off:off + w], KA[r][a][:, kb * T:(kb + 1) * T],
                                          QA[r][a][:, q0:q0 + w], start=True, stop=False)
                                ins = pe.matmul(bank[:, off:off + w], KB[r][a][0:D + 2, kb * T:(kb + 1) * T],
                                                QB[r][a][0:D + 2, q0:q0 + w], start=False, stop=True)
                                if kb * T >= q0:
                                    ins = pe.matmul(bank[:, off:off + T], maskb[:, :], identb[:, :],
                                                    start=False, stop=True, skip_group_check=True)
                                off += w
                            ins.then_inc(st_full, 1)
                        elif kind == "pv":
                            n = a * 4 + c
                            head = 2 * p + a
                            bank = PV
                            pe.wait_ge(st_free, 3 + (gp * 2 + a) * NU + (3 if c < 2 else NU))
                            pe.wait_ge(pv_free, gp * 8 + n + 1)
                            for i in range(2):
                                qt = 2 * c + i
                                o = i * (2 * D + 1)
                                for kb in range(qt + 1):
                                    pu, q = block_at(kb, qt)
                                    pe.matmul(bank[:, o:o + 2 * D + 1], P[:, pu, 0, q:q + T],
                                              V[:, kb, head, 0:2 * D + 1], start=(kb == 0), stop=False,
                                              skip_group_check=True)
                                    ins = pe.matmul(bank[:, o:o + D + 1], P[:, pu, 1, q:q + T],
                                                    V[:, kb, head, 0:D + 1], start=False, stop=(kb == qt),
                                                    skip_group_check=True)
                            ins.then_inc(pv_full, 1)
                        elif kind == "proj":
                            if a == 0 and c == 0:
                                pe.wait_ge(w_dma[1 - r], (b * (PAIRS // 2) + turn + r + 1) * 32)
                            proj(a, c, 1 - r, gp + 1)
                        elif kind == "max":
                            if a == 2:
                                for s, count in MAX_NEEDS.get(c, []):
                                    pe.wait_ge(stage_dma[s], 64 + (gp + 1) * 128 + count)
                            maxima(a % 2, c, r if a == 1 else 1 - r, bank, free)
                        elif kind == "mt":
                            max_transpose(a % 2, bank, free, gp * 2 + a + 1)
                        elif kind == "xf":
                            pe.wait_ge(work_free, free)
                            x_rows(a, r, bank, (b + 1) * NT + p)
                        elif kind == "xb":
                            pe.wait_ge(work_free, free)
                            x_quantised(bank, (b + 1) * NT + p)
                        elif kind == "ot":
                            pe.wait_ge(o_done, 2 + gp * 8 + 4 + a // 2 + 1)
                            pe.wait_ge(work_free, free)
                            for i in range(2):
                                ins = pe.transpose(bank[:, i * T:(i + 1) * T], ost[:, a + i, :], ident[:, :])
                            ins.then_inc(work_full, 1)
                        u += is_unit(step)

                pairs(pe, pair)
                pe.wait_ge(wo_dma, (b + 1) * 16)
                pe.wait_ge(work_free, base + 3 + nu.at_out)
                for t in range(NT):
                    for half in range(2):
                        u = nu.at_out + 2 * t + half
                        pe.wait_ge(work_free, base + u + 1)
                        split_product(WK[(W_PRO + u) % 3], PAIRS,
                                      lambda l, k: OT[:, l, k, t * T:(t + 1) * T],
                                      lambda l, k: WO[:, 4 * half:4 * half + 4, l, k, :]).then_inc(work_full, 1)

            batches(pe, batch)

        @block.scalar
        def _(act):
            def x_scaled(k, slot):
                act.wait_ge(xn_ready, k + 1)
                if not (isinstance(k, int) and k == 0):
                    act.wait_ge(q_done, k)
                act.activation(qy, xt[slot], ACT.Copy, scale=s_("scale_x")).then_inc(q_y, 1)

            def x_hi(k, g, bank, full):
                act.wait_ge(work_full, full)
                if g == 0 and not (isinstance(k, int) and k == 0):
                    act.wait_ge(xs_st, k * 16)
                act.activation(xst[:, 0, 4 * g:4 * g + 4, :], bank[:, :].rearrange("p (k f) -> p k f", k=4),
                               ACT.Copy).then_inc(work_hi, 1)

            act.wait_ge(sc_ready, 1)
            for t in range(NT):
                x_scaled(t, t % 2)
                for g in range(2):
                    n = 1 + 3 * t + g
                    x_hi(t, g, WK[n % 3], n + 1)
            act.wait_ge(sc_ready, 2)
            for i, w in enumerate(W_ORDER):
                m = w // NT
                if i % W2_EVERY == 0 and i // W2_EVERY < NT:
                    t = i // W2_EVERY
                    act.wait_ge(w2_dma, 16 * (t + 1))
                    if t >= 2:
                        act.wait_ge(w2_done, t - 1)
                    act.activation(w2y[t % 2], w2t, ACT.Copy, scale=s_("scale1")).then_inc(w2_y, 1)
                for g in range(2):
                    n = 1 + 3 * NT + 2 * i + g
                    act.wait_ge(work_full, n + 1)
                    if i >= 4:
                        act.wait_ge(w_st[i % 4], 16 * (i // 4))
                    act.activation(wst[:, i % 4, 0, 4 * g:4 * g + 4, :],
                                   WK[n % 3][:, :].rearrange("p (k f) -> p k f", k=4), ACT.Copy,
                                   scale=s_("w_s", 4)[:, m:m + 1]).then_inc(work_hi, 1)

            def rows_to_stack(h, r, k):
                until(act, work_free, k)
                for part in range(2):
                    act.dma_start(QB[r][h][D + part:D + part + 1, :], m_hl[:, h, part, :]).then_inc(m_dma[h], 16)

            def batch(b, with_x):
                nu = U[with_x]
                base = b * U[1].all + W_PRO

                def proj(n, gp):
                    s = n % 2
                    until(act, stage_dma[s], 64 + gp * 128 + (n // 2) * 64)
                    act.wait_ge(pj_free, 1 + gp * 4 + n + 1)
                    act.activation(stage[:, s, 0, :], qk32[s], ACT.Copy).then_inc(pj_hi, 1)

                def max_rows(h, full, bank, gp):
                    act.wait_ge(work_full, full)
                    act.wait_ge(m_dma[h], 32 + gp * 32)
                    act.activation(m_hl[:, h, 0, :], bank[0:NT, 0:T], ACT.Copy, scale=1.0 / SHIFT)\
                       .then_inc(work_hi, 1)

                u = 0
                for step in first_steps():
                    kind, a, c = step
                    bank = WK[(W_PRO + u) % 3]
                    full = base + u + 1
                    if kind == "v":
                        act.wait_ge(work_full, full)
                        act.activation(V[:, a, 8 * c:8 * c + 8, 0:D], bank[:, :].rearrange("p (h d) -> p h d", d=D),
                                       ACT.Copy, scale=s_("c_v")).then_inc(work_hi, 1)
                    elif kind == "proj" and c == SEGS - 1:
                        proj(a, b * PAIRS)
                    elif kind == "mt":
                        max_rows(0, full, bank, b * PAIRS)
                        mt_unit = base + 3 + u + 1
                    elif kind == "mr":
                        rows_to_stack(0, 0, mt_unit)
                    u += is_unit(step)

                def pair(p, r, turn, with_next, more):
                    gp = b * PAIRS + p
                    u = 0
                    for step in pair_steps(with_next, with_x):
                        kind, a, c = step
                        bank = WK[(W_PRO + nu.first + u) % 3]
                        full = base + nu.first + p * nu.pair + u + 1
                        if kind == "st":
                            n = a * NU + c
                            act.wait_ge(st_full, 1 + gp * 2 * NU + n + 1)
                            if c == 0:
                                act.wait_ge(pv_full, 2 + (gp * 2 + a) * 4)
                            if c == 2:
                                act.wait_ge(pv_full, 4 + (gp * 2 + a) * 4)
                            act.activation(P[:, c, 0, :], ST[n % 3][:, :], ACT.Exp, scale=s_("e_s"))
                            act.activation(ST[n % 3][:, :], ST[n % 3][:, :], ACT.Exp, scale=s_("e_s"))\
                               .then_inc(st_exp, 1)
                        elif kind == "pv":
                            n = a * 4 + c
                            act.wait_ge(pv_full, 4 + gp * 8 + n + 1)
                            src = PV[:, 0:2 * (2 * D + 1)].rearrange("p (i w) -> p i w", i=2)
                            act.activation(pv_lo[:, n % 2, :, :], src[:, :, D + 1:2 * D + 1], ACT.Copy)\
                               .then_inc(pv_half, 1)
                        elif kind == "proj" and c == SEGS - 1:
                            proj(a, gp + 1)
                        elif kind == "mt":
                            max_rows(a % 2, full, bank, gp + a // 2)
                            mt_unit = full + 3
                        elif kind == "mr":
                            rows_to_stack(a % 2, r if a == 1 else 1 - r, mt_unit)
                        elif kind == "xn":
                            x_scaled((b + 1) * NT + p, r)
                        elif kind == "xf":
                            x_hi((b + 1) * NT + p, a, bank, full)
                        elif kind == "ot":
                            until(act, work_full, full)
                            act.activation(OT[:, 0, p, a * T:(a + 2) * T], bank[:, 0:2 * T], ACT.Identity,
                                           bias=bias[:, 2, at(p)]).then_inc(work_hi, 1)
                        u += is_unit(step)

                pairs(act, pair)

            batches(act, batch)

        @block.vector
        def _(v):
            me = Chain(v, dve)

            def rounding(y, m, done):
                me.step(v.tensor_scalar(m.bitcast(u32), y.bitcast(u32), 0x7F800000, None, ALU.bitwise_and))
                v.tensor_scalar(m, m, 2.0 ** -6, 1.5 * 2.0 ** 20, ALU.max, ALU.mult).then_inc(done, 1)

            X_CHAIN = 4

            def x_statistics(k, turn, slot):
                a, stats = xt[slot], s_("stats", 12)
                v.wait_ge(x_dma[slot], 16 * (turn + 1))
                v.bn_stats(stats[:, 0:6], a[:, 0:CH])
                me.step(v.bn_stats(stats[:, 6:12], a[:, CH:H]))
                v.sem_inc(held, 1)
                me.step(v.bn_aggr(s_("mv", 2), stats))
                v.tensor_scalar(s_("var"), s_("mv", 2)[:, 1:2], 1e-5, None, ALU.add).then_inc(var_ready, 1)

            def x_normalised(k, slot):
                v.wait_ge(rstd_ready, k + 1)
                me.step(v.tensor_scalar(s_("rs10"), s_("rstd"), 2.0 ** 10, None, ALU.mult))
                v.tensor_scalar(xt[slot], xt[slot], s_("mv", 2)[:, 0:1], s_("rs10"), ALU.subtract, ALU.mult)\
                 .then_inc(xn_ready, 1)

            def x_rounding(k):
                v.wait_ge(q_y, k + 1)
                rounding(qy, qm, q_m)

            def x_lo(g, bank, hi_n):
                v.wait_ge(work_hi, hi_n)
                hi, lo = (xst[:, l, 4 * g:4 * g + 4, :] for l in range(2))
                v.tensor_tensor(lo, bank[:, :].rearrange("p (k f) -> p k f", k=4), hi, ALU.subtract)\
                 .then_inc(work_free, 1)

            def x_quantised(k, bank, full):
                v.wait_ge(work_full, full)
                if not (isinstance(k, int) and k == 0):
                    v.wait_ge(xq_st, k * 16)
                v.tensor_copy(xqs, bank[:, :].bitcast(bf16)).then_inc(work_free, 1)

            v.memset(m_part[:, :, :, :], NEG)
            v.sem_inc(work_free, 3)
            v.sem_inc(st_free, 3)
            v.sem_inc(st_full, 1)
            v.sem_inc(pv_full, 4)
            v.sem_inc(pv_free, 1)
            v.sem_inc(pj_free, 1)
            for i in range(2):
                v.sem_inc(out_st[i], 16)
                for q in y_st[i]:
                    v.sem_inc(q, 16)
                v.sem_inc(stage_dma[i], 64)
                v.sem_inc(m_dma[i], 32)

            v.wait_ge(misc_dma, 48)
            v.tensor_scalar(s_("scale_x"), s_("scale"), 2.0 ** -10, None, ALU.mult).then_inc(sc_ready, 1)
            mx = s_("mx", 7)
            v.wait_ge(work_full, 1)
            me.step(v.tensor_copy(bias[:, :, :].rearrange("p a n -> p (a n)"), WK[0][:, 0:24]))
            v.tensor_reduce(mx[:, 4:7], bias[:, :, :], AX.X, ALU.max, apply_absolute_value=True)\
             .then_inc(work_free, 1)

            rmx = s_("rmx", 4 * NT)

            def raw_maxima(t, g):
                if g == 0:
                    v.wait_ge(raw_dma[t], 64)
                return v.tensor_reduce(rmx[:, NT * g + t:NT * g + t + 1], raw[NT * g + t], AX.X, ALU.max,
                                       apply_absolute_value=True)

            x_statistics(0, 0, 0)
            for t in range(NT):
                x_normalised(t, t % 2)
                if t + 1 < NT:
                    x_statistics(t + 1, (t + 1) // 2, (t + 1) % 2)
                if t >= 1:
                    n = 1 + 3 * (t - 1) + 2
                    x_quantised(t - 1, WK[n % 3], n + 1)
                    raw_maxima(t - 1, 0)
                    raw_maxima(t - 1, 1)
                x_rounding(t)
                for g in range(2):
                    n = 1 + 3 * t + g
                    x_lo(g, WK[n % 3], 2 * t + g + 1)
                    if t >= 1:
                        raw_maxima(t - 1, 2 + g)
            for g in range(4):
                ins = raw_maxima(NT - 1, g)
            me.step(ins)
            v.tensor_reduce(mx[:, 0:4], rmx.rearrange("p (g t) -> p g t", g=4), AX.X, ALU.max)\
             .then_inc(mx_ready, 1)
            x_quantised(NT - 1, WK[(3 * NT) % 3], 3 * NT + 1)
            v.wait_ge(gmax, 1)
            g = s_("g", 7)
            bd, eb, ew, e1, e2 = s_("bd", 3), s_("eb", 3), s_("ew", 4), s_("e1"), s_("e2")
            me.step(v.tensor_scalar(g, g, 2.0 ** -100, 2.0 ** 100, ALU.max, ALU.min))
            me.step(v.tensor_scalar(g[:, 0:2], g[:, 0:2], 2.0 ** -20, None, ALU.max))
            me.step(v.scalar_tensor_tensor(out=bd, in0=g[:, 0:3], scalar=1024.0, in1=g[:, 4:7],
                                           op0=ALU.mult, op1=ALU.add))
            me.step(v.tensor_scalar(eb.bitcast(u32), bd.bitcast(u32), 0x7F800000, None, ALU.bitwise_and))
            me.step(v.tensor_scalar(ew.bitcast(u32), g[:, 0:4].bitcast(u32), 0x7F800000, None, ALU.bitwise_and))

            def power(dst, src, e):
                return v.tensor_scalar(dst.bitcast(u32), src.bitcast(u32), -1.0, float((254 + e) << 23),
                                       ALU.mult, ALU.add)
            ss = s_("ss", 3)
            me.step(power(s_("w_s", 4), ew, 13))
            me.step(power(ss[:, 0:2], eb[:, 0:2], 11))
            me.step(power(ss[:, 2:3], eb[:, 2:3], 14))
            me.step(v.tensor_scalar(ew, ew, 2.0 ** -23, None, ALU.mult))
            for i, nm in enumerate(("c_q", "c_k", "c_v")):
                me.step(v.tensor_tensor(s_(nm), ss[:, i:i + 1], ew[:, i:i + 1], ALU.mult))
                me.step(v.tensor_scalar(bias[:, i, :], bias[:, i, :], ss[:, i:i + 1], None, ALU.mult))
            me.step(v.tensor_scalar(e1, eb[:, 0:1], 2.0 ** -11, None, ALU.mult))
            me.step(v.scalar_tensor_tensor(out=s_("e_s"), in0=eb[:, 1:2], scalar=2.0 ** -11 * D ** -0.5,
                                           in1=e1, op0=ALU.mult, op1=ALU.mult))
            me.step(v.tensor_scalar(e2, eb[:, 2:3], 2.0 ** -14 * 2.0 ** 10, None, ALU.mult))
            me.step(v.tensor_tensor(s_("c_o"), e2, ew[:, 3:4], ALU.mult))
            me.step(v.reciprocal(e1, s_("scale")))
            me.step(v.reciprocal(e2, s_("scale1")))
            v.tensor_tensor(s_("c_f"), e1, e2, ALU.mult).then_inc(sc_ready, 1)

            for i, w in enumerate(W_ORDER):
                m = w // NT
                if i % W2_EVERY == 1 and i // W2_EVERY < NT:
                    v.wait_ge(w2_y, i // W2_EVERY + 1)
                    rounding(w2y[i // W2_EVERY % 2], w2m[i // W2_EVERY % 2], w2_m)
                for g2 in range(2):
                    n = 1 + 3 * NT + 2 * i + g2
                    v.wait_ge(work_hi, 2 * NT + 2 * i + g2 + 1)
                    hi, lo = (wst[:, i % 4, l, 4 * g2:4 * g2 + 4, :] for l in range(2))
                    v.scalar_tensor_tensor(out=lo, in0=WK[n % 3][:, :].rearrange("p (k f) -> p k f", k=4),
                                           scalar=s_("w_s", 4)[:, m:m + 1], in1=hi,
                                           op0=ALU.mult, op1=ALU.subtract).then_inc(work_free, 1)
            v.memset(V[:, :, :, D:D + 1], 1.0)
            for r in range(2):
                for h in range(2):
                    v.memset(KB[r][h][D:D + 2, :], SHIFT)
            chain0 = me.n

            def batch(b, with_x):
                nu, nh = U[with_x], HI[with_x]
                base = b * U[1].all + W_PRO
                hbase = b * HI[1].all + HI_PRO

                def proj(n, gp, p):
                    v.wait_ge(pj_full, gp * 4 + n + 1)
                    v.wait_ge(pj_lo, gp * 4 + n + 1)
                    kind = PROJ_UNITS[n][0]
                    v.tensor_scalar(qk32[n % 2], PJ[:, :], s_(("c_q", "c_k")[kind]),
                                    bias[:, kind, at(p)], ALU.mult, ALU.add).then_inc(pj_free, 1)

                def maxima(h, u, bank, full):
                    v.wait_ge(work_full, full)
                    off = 0
                    for qt, k, w in MAX_UNITS[u]:
                        ins = v.tensor_reduce(m_part[:, h, qt, k // CH:k // CH + 1],
                                              bank[:, off:off + w], AX.X, ALU.max)
                        off += w
                    ins.then_inc(work_free, 1)
                    if u == NU - 1:
                        v.wait_ge(work_free, full + 3)
                        v.tensor_reduce(m_neg[:, h, :], m_part[:, h, :, :], AX.X, ALU.max,
                                        negate=True).then_inc(m_ready, 1)

                def max_rows(h, bank, hi_n):
                    v.wait_ge(work_hi, hi_n)
                    v.scalar_tensor_tensor(out=m_hl[:, h, 1, :], in0=bank[0:NT, 0:T],
                                           scalar=1.0 / SHIFT, in1=m_hl[:, h, 0, :],
                                           op0=ALU.mult, op1=ALU.subtract).then_inc(work_free, 1)

                u = hi = 0
                for step in first_steps():
                    kind, a, c = step
                    bank = WK[(W_PRO + u) % 3]
                    full = base + u + 1
                    hi += has_hi(step)
                    if kind == "ffn":
                        if c == 0:
                            v.wait_ge(xb_ready, b * NT + a + 1)
                        v.wait_ge(work_full, full)
                        v.wait_ge(y_st[a % 2][c], 16 + b * NT * 8 + (a // 2) * 16)
                        v.scalar_tensor_tensor(out=yst[a % 2][c], in0=bank[:, :], scalar=s_("c_f"),
                                               in1=xr[a % 3][:, c * CH:(c + 1) * CH],
                                               op0=ALU.mult, op1=ALU.add).then_inc(work_free, 1)
                    elif kind == "v":
                        v.wait_ge(work_hi, hbase + hi)
                        vh, vl = (V[:, a, 8 * c:8 * c + 8, o:o + D] for o in (0, D + 1))
                        v.scalar_tensor_tensor(out=vl, in0=bank[:, :].rearrange("p (h d) -> p h d", d=D),
                                               scalar=s_("c_v"), in1=vh,
                                               op0=ALU.mult, op1=ALU.subtract).then_inc(work_free, 1)
                    elif kind == "proj" and c == SEGS - 1:
                        proj(a, b * PAIRS, 0)
                    elif kind == "max":
                        maxima(0, c, bank, full)
                    elif kind == "mt":
                        max_rows(0, bank, hbase + hi)
                    u += is_unit(step)

                def pair(p, r, turn, with_next, more):
                    gp = b * PAIRS + p
                    tile = (b + 1) * NT + p
                    me.base, me.n = chain0 + (b * NT + p) * X_CHAIN, 0
                    u = hi = 0
                    for step in pair_steps(with_next, with_x):
                        kind, a, c = step
                        bank = WK[(W_PRO + nu.first + u) % 3]
                        full = base + nu.first + p * nu.pair + u + 1
                        hi += has_hi(step)
                        hi_n = hbase + nh.first + p * nh.pair + hi
                        if kind == "st":
                            n = a * NU + c
                            v.wait_ge(st_exp, gp * 2 * NU + n + 1)
                            v.tensor_tensor(P[:, c, 1, :], ST[n % 3][:, :], P[:, c, 0, :],
                                            ALU.subtract).then_inc(st_free, 1)
                        elif kind == "pv":
                            n = a * 4 + c
                            src = PV[:, 0:2 * (2 * D + 1)].rearrange("p (i w) -> p i w", i=2)
                            v.wait_ge(o_done, gp * 8 + n + 1)
                            v.wait_ge(pv_half, gp * 8 + n + 1)
                            v.reciprocal(pv_rec[:, n % 2, :, :], src[:, :, D:D + 1])
                            v.tensor_tensor(pv_num[:, n % 2, :, :], src[:, :, 0:D], pv_lo[:, n % 2, :, :],
                                            ALU.add).then_inc(pv_free, 1)
                        elif kind == "proj" and c == SEGS - 1:
                            proj(a, gp + 1, p + 1)
                        elif kind == "max":
                            maxima(a % 2, c, bank, full)
                        elif kind == "mt":
                            max_rows(a % 2, bank, hi_n)
                        elif kind == "xs":
                            x_statistics(tile, (b + 1) * (NT // 2) + turn, r)
                        elif kind == "xn":
                            x_normalised(tile, r)
                        elif kind == "xm":
                            x_rounding(tile)
                        elif kind == "xf":
                            x_lo(a, bank, hi_n)
                        elif kind == "xb":
                            x_quantised(tile, bank, full)
                        elif kind == "ot":
                            v.wait_ge(work_hi, hi_n)
                            lo, hi_part = (OT[:, l, p, a * T:(a + 2) * T] for l in (1, 0))
                            v.scalar_tensor_tensor(out=lo, in0=bank[:, 0:2 * T], scalar=bias[:, 2, at(p)], in1=hi_part,
                                                   op0=ALU.add, op1=ALU.subtract).then_inc(work_free, 1)
                        u += is_unit(step)

                pairs(v, pair)
                for t in range(NT):
                    for half in range(2):
                        u = nu.at_out + 2 * t + half
                        v.wait_ge(work_full, base + u + 1)
                        v.wait_ge(y_dma[t % 2], b * 64 + 16 * (t // 2 + 1))
                        y = yt[t % 2][:, half * CH:(half + 1) * CH]
                        v.scalar_tensor_tensor(out=y, in0=WK[(W_PRO + u) % 3][:, :], scalar=s_("c_o"),
                                               in1=y, op0=ALU.mult, op1=ALU.add).then_inc(work_free, 1)

            batches(v, batch)

        @block.gpsimd
        def _(g):
            me = Chain(g, pool)
            g.sem_inc(o_done, 2)
            g.sem_inc(pj_lo, 2)
            g.memset(s_("half"), -0.5).then_inc(consts, 1)
            me.step(g.memset(ident[:, :], 0.0))
            g.affine_select(out=ident[:, :], in_=ident[:, :], compare_op=ALU.not_equal, fill=1.0, base=0,
                            pattern=[[-1, T]], channel_multiplier=1).then_inc(consts, 1)
            me.step(g.memset(identb[:, :], 0.0))
            g.affine_select(out=identb[:, :], in_=identb[:, :], compare_op=ALU.not_equal, fill=1.0, base=0,
                            pattern=[[-1, T]], channel_multiplier=1).then_inc(consts, 1)
            me.step(g.memset(maskb[:, :], 0.0))
            g.affine_select(out=maskb[:, :], in_=maskb[:, :], compare_op=ALU.is_ge, fill=NEG, base=0,
                            pattern=[[-1, T]], channel_multiplier=1).then_inc(consts, 2)

            Q_CHAIN = 3

            def quantise(k, ready, done, y, m, q, dst, stored=None):
                g.wait_ge(ready, k + 1)
                me.step(g.tensor_tensor(y, y, m, ALU.add))
                me.step(g.tensor_tensor(q, y, m, ALU.subtract))
                g.sem_inc(held, 1)
                me.step(g.tensor_scalar(y, q, 2.0 ** 119 * 1.125, 0.0, ALU.mult, ALU.mult))
                if stored is not None:
                    g.wait_ge(*stored)
                g.tensor_tensor(dst, q, y, ALU.add).then_inc(done, 1)

            def x_rstd(k):
                g.wait_ge(var_ready, k + 1)
                g.tensor_tensor(s_("rstd"), s_("var"), s_("half"), ALU.pow).then_inc(rstd_ready, 1)

            x_rstd(0)
            for t in range(NT):
                if t + 1 < NT:
                    x_rstd(t + 1)
                if t >= 1:
                    g.wait_ge(work_full, 1 + 3 * t)
                quantise(t, q_m, q_done, qy, qm, qq, xqt)
            g.wait_ge(mx_ready, 1)
            g.partition_all_reduce(s_("g", 7), s_("mx", 7), T, bass.bass_isa.ReduceOp.max).then_inc(gmax, 1)
            for t in range(NT):
                quantise(t, w2_m, w2_done, w2y[t % 2], w2m[t % 2], w2q32, w2b,
                         (w2_st, 16 * t) if t >= 1 else None)
            chain0 = me.n

            def batch(b, with_x):
                nu = U[with_x]
                base = b * U[1].all + W_PRO
                g.wait_ge(bout_dma, (b + 1) * 16)
                for t in range(NT):
                    g.wait_ge(xr_dma[t % 3], b * (48, 48, 32)[t % 3] + 16 * (t // 3 + 1))
                    g.tensor_tensor(xr[t % 3], xr[t % 3], bout, ALU.add).then_inc(xb_ready, 1)

                for q in y_st[1]:
                    until(g, q, 16 + (b + 1) * NT * 8)

                def proj(n, gp):
                    g.wait_ge(pj_hi, gp * 4 + n + 1)
                    g.tensor_tensor(stage[:, n % 2, 1, :], qk32[n % 2], stage[:, n % 2, 0, :],
                                    ALU.subtract).then_inc(pj_lo, 1)

                for kind, a, c in first_steps():
                    if kind == "proj" and c == SEGS - 1:
                        proj(a, b * PAIRS)

                def pair(p, r, turn, with_next, more):
                    gp = b * PAIRS + p
                    me.base, me.n = chain0 + (b * NT + p) * Q_CHAIN, 0
                    for kind, a, c in pair_steps(with_next, with_x):
                        if kind == "proj" and c == SEGS - 1:
                            proj(a, gp + 1)
                        if kind == "pv":
                            n = a * 4 + c
                            g.wait_ge(pv_free, 1 + gp * 8 + n + 1)
                            if n == 0:
                                g.wait_ge(work_full, base + nu.first + p * nu.pair)
                            dst = ost[:, 2 * c:2 * c + 2, a * D:(a + 1) * D]
                            g.tensor_tensor(dst, pv_num[:, n % 2, :, :],
                                            pv_rec[:, n % 2, :, :].to_broadcast((T, 2, D)),
                                            ALU.mult).then_inc(o_done, 1)
                        elif kind == "xs":
                            x_rstd((b + 1) * NT + p)
                        elif kind == "xm":
                            g.wait_ge(work_full, base + nu.first + p * nu.pair)
                            quantise((b + 1) * NT + p, q_m, q_done, qy, qm, qq, xqt)

                pairs(g, pair)

            batches(g, batch)


_INS = ['L0_attn_x', 'L0_attn_W_qkv', 'L0_attn_b_qkv', 'L0_attn_W_out', 'L0_attn_b_out',
        'L0_ffn_input2', 'L0_ffn_scale', 'L0_ffn_scale1']
_OUTS = [((B, S, H), 'float32')]


def kernel(**inputs):
    import numpy as _np
    import concourse.bacc as _bacc
    from concourse import mybir as _mybir
    from concourse.bass_utils import run_bass_kernel_spmd as _run

    nc = _bacc.Bacc("TRN2", target_bir_lowering=False, num_devices=1)
    arrays, args = {}, []
    for name in _INS:
        a = _np.ascontiguousarray(inputs[name])
        if a.ndim == 0:
            a = a.reshape(1, 1)
        arrays[f"in_{name}_dram"] = a
        args.append(nc.dram_tensor(f"in_{name}_dram", a.shape, _mybir.dt.from_np(a.dtype), kind="ExternalInput").ap())
    for i, (shape, dtype) in enumerate(_OUTS):
        dt = _mybir.dt.from_np(_np.dtype(dtype))
        args.append(nc.dram_tensor(f"out_{i}_dram", shape, dt, kind="ExternalOutput").ap())
    block_kernel(nc, *args)
    r = _run(nc, [arrays], core_ids=[0])
    got = tuple(r.results[0][f"out_{i}_dram"] for i in range(len(_OUTS)))
    return got[0]
```
